# Optimizing a Trainium2 kernel written in Bass

```python
import numpy as np
import jax
import jax.numpy as jnp

def _softmax(x, axis=-1):
    return jax.nn.softmax(x, axis=axis)

def _gelu(x):
    return jax.nn.gelu(x, approximate=True)

def _silu(x):
    return jax.nn.silu(x)

def _sigmoid(x):
    return jax.nn.sigmoid(x)

def _layernorm(x, axis=-1, eps=1e-05):
    m = jnp.mean(x, axis=axis, keepdims=True)
    v = jnp.var(x, axis=axis, keepdims=True)
    return (x - m) / jnp.sqrt(v + eps)

def _scatter_add(tgt, idx, src, axis=0):
    return tgt.at[idx].add(src)

def _segment_sum(src, seg, n):
    return jax.ops.segment_sum(src, seg, n)
kernel_name = 'mk_macaron_d1_jaxref_r8_198225'

def setup_inputs(seed: int=0):
    np.random.seed(seed)
    _w = jnp.asarray

    def _L0_attn_setup():
        import jax, jax.numpy as jnp
        import numpy as np
        EMBED = 128
        HEADS = 16
        HEAD_DIM = EMBED // HEADS
        key = jax.random.key(seed)
        k1, k2, k3, k4, k5 = jax.random.split(key, 5)
        scale = 1.0 / np.sqrt(EMBED)
        return {'x': jax.random.normal(k1, (4, 256, EMBED), dtype=jnp.float32), 'qkv_w': jax.random.uniform(k2, (3 * EMBED, EMBED), minval=-scale, maxval=scale, dtype=jnp.float32), 'qkv_b': jax.random.uniform(k3, (3 * EMBED,), minval=-scale, maxval=scale, dtype=jnp.float32), 'out_w': jax.random.uniform(k4, (EMBED, EMBED), minval=-scale, maxval=scale, dtype=jnp.float32), 'out_b': jax.random.uniform(k5, (EMBED,), minval=-scale, maxval=scale, dtype=jnp.float32)}
    _L0_attn_in = _L0_attn_setup()

    def _L0_ffn_setup():
        import jax, jax.numpy as jnp
        import numpy as np
        DIM = 128
        HIDDEN = 384
        SCALE = 1.0 / 127.0

        def _dequant(w_int, dtype):
            return w_int.astype(dtype) * jnp.asarray(SCALE, dtype)
        key = jax.random.key(seed)
        k_x, k_g, k_u, k_d = jax.random.split(key, 4)
        x = jax.random.normal(k_x, (4, 256, DIM), dtype=jnp.float32)
        w_gate = jax.random.randint(k_g, (HIDDEN, DIM), -127, 128, dtype=jnp.int32)
        w_up = jax.random.randint(k_u, (HIDDEN, DIM), -127, 128, dtype=jnp.int32)
        w_down = jax.random.randint(k_d, (DIM, HIDDEN), -127, 128, dtype=jnp.int32)
        return {'x': x, 'w_gate': w_gate, 'w_up': w_up, 'w_down': w_down}
    _L0_ffn_in = _L0_ffn_setup()
    _d = {'L0_attn_x': _L0_attn_in['x'], 'L0_attn_qkv_w': _L0_attn_in['qkv_w'], 'L0_attn_qkv_b': _L0_attn_in['qkv_b'], 'L0_attn_out_w': _L0_attn_in['out_w'], 'L0_attn_out_b': _L0_attn_in['out_b'], 'L0_ffn_w_gate': _L0_ffn_in['w_gate'], 'L0_ffn_w_up': _L0_ffn_in['w_up'], 'L0_ffn_w_down': _L0_ffn_in['w_down']}
    _x0 = _d['L0_attn_x']
    _d['L0_attn_x'] = jax.random.normal(jax.random.fold_in(jax.random.key(seed), 1), (4, 1024, 128), dtype=_x0.dtype)
    del _x0
    return _d

def reference(L0_attn_x, L0_attn_qkv_w, L0_attn_qkv_b, L0_attn_out_w, L0_attn_out_b, L0_ffn_w_gate, L0_ffn_w_up, L0_ffn_w_down):

    def _L0_attn_ref(x, qkv_w, qkv_b, out_w, out_b):
        import jax, jax.numpy as jnp
        import numpy as np
        EMBED = 128
        HEADS = 16
        HEAD_DIM = EMBED // HEADS
        b, n, _ = x.shape
        qkv = (jnp.einsum('bne,fe->bnf', x, qkv_w) + qkv_b).reshape(b, n, 3, HEADS, HEAD_DIM)
        q, k, v = (qkv[:, :, 0], qkv[:, :, 1], qkv[:, :, 2])
        scores = jnp.einsum('bnhd,bmhd->bhnm', q, k) / jnp.sqrt(jnp.float32(HEAD_DIM))
        attn = jax.nn.softmax(scores, axis=-1)
        out = jnp.einsum('bhnm,bmhd->bnhd', attn, v).reshape(b, n, EMBED)
        return jnp.einsum('bne,fe->bnf', out, out_w) + out_b

    def _L0_ffn_ref(x, w_gate, w_up, w_down):
        import jax, jax.numpy as jnp
        import numpy as np
        DIM = 128
        HIDDEN = 384
        SCALE = 1.0 / 127.0

        def _dequant(w_int, dtype):
            return w_int.astype(dtype) * jnp.asarray(SCALE, dtype)
        wg = _dequant(w_gate, x.dtype)
        wu = _dequant(w_up, x.dtype)
        wd = _dequant(w_down, x.dtype)
        gate = jnp.einsum('bsd,hd->bsh', x, wg)
        up = jnp.einsum('bsd,hd->bsh', x, wu)
        h = jax.nn.silu(gate) * up
        return jnp.einsum('bsh,dh->bsd', h, wd)
    x = L0_attn_x
    x = x + 0.5 * _L0_ffn_ref(_layernorm(x, axis=-1), L0_ffn_w_gate, L0_ffn_w_up, L0_ffn_w_down)
    x = x + _L0_attn_ref(_layernorm(x, axis=-1), L0_attn_qkv_w, L0_attn_qkv_b, L0_attn_out_w, L0_attn_out_b)
    x = x + 0.5 * _L0_ffn_ref(_layernorm(x, axis=-1), L0_ffn_w_gate, L0_ffn_w_up, L0_ffn_w_down)
    return x

_drawn_inputs = setup_inputs


def setup_inputs(seed=0):
    import zlib

    import numpy as np

    out = dict(_drawn_inputs(seed))
    spreads = {}
    factors = {'L0_attn_qkv_w': 8.0, 'L0_attn_qkv_b': 8.0, 'L0_attn_out_w': 8.0, 'L0_attn_out_b': 64.0}
    for name, (base, spread) in spreads.items():
        noise = np.random.default_rng([zlib.crc32(name.encode()), seed]).standard_normal(out[name].shape)
        drawn = base * np.exp(spread * noise) if base else spread * noise
        out[name] = jnp.asarray(drawn.astype(out[name].dtype))
    for name, factor in factors.items():
        out[name] = (out[name] * factor).astype(out[name].dtype)
    return out
```

```python
from contextlib import ExitStack

import concourse.bass as bass
from concourse import mybir

ALU = mybir.AluOpType
ACT = mybir.ActivationFunctionType
AX = mybir.AxisListType
F32 = mybir.dt.float32
BF16 = mybir.dt.bfloat16
I32 = mybir.dt.int32

P = 128
BATCH, SEQ, DIM = 4, 1024, 128
HEADS = 16
DH = DIM // HEADS
HID = 384
SCALE_INT8 = 1.0 / 127.0
SCALE_QK = float(DH) ** -0.5
EPS = 1e-5

ROWS = BATCH * SEQ
TILES = ROWS // P
BLK = 512
BT = BLK // P
NBLK = ROWS // BLK
CH = HID // P
HP = HEADS // 2
PAIRS = BATCH * HP
UQ = 512
KT = SEQ // P
STEPS = KT // 2
PARTS = 3
QK_ROWS = PARTS * PARTS * DH
ALL_ROWS = QK_ROWS + PARTS
NBUF = 3
VW = 32
LOADS = 2 * 2 * PARTS


def past(count):
    return not isinstance(count, int) or count > 0


def run_blocks(eng, step):
    step(0, 0, 0)
    step(1, 1, 0)
    with eng.Fori(1, NBLK // 2 - 1) as i:
        step(2 * i, 0, i)
        step(2 * i + 1, 1, i)
    step(NBLK - 2, 0, NBLK // 2 - 1)
    step(NBLK - 1, 1, NBLK // 2 - 1)


def run_pairs(eng, step, head, turns=9):
    for p in range(head):
        step(p, p % NBUF, p // NBUF)
    with eng.Fori(0, turns) as i:
        for k in range(head, head + NBUF):
            step(i * NBUF + k, k % NBUF, i + k // NBUF)
    for p in range(head + turns * NBUF, PAIRS):
        step(p, p % NBUF, p // NBUF)


def macaron(nc, x_in, wqkv_t, qkv_b, wo_t, out_b, wg_t, wu_t, wd_t, out):
    with ExitStack() as ctx:
        def sb(name, shape, dt):
            return ctx.enter_context(nc.sbuf_tensor(name, shape, dt))

        def psum(name, shape):
            return ctx.enter_context(nc.psum_tensor(name, shape, F32))

        def sem(name):
            return ctx.enter_context(nc.semaphore(name))

        q_scr = nc.dram_tensor("q_parts_scratch", [PAIRS, PARTS, 2, DH, SEQ], BF16).ap()
        k_scr = nc.dram_tensor("k_parts_scratch", [PAIRS, PARTS, 2, DH, SEQ], BF16).ap()

        x = sb("x", [P, TILES, DIM], F32)
        stats = sb("stats", [P, TILES, 6], F32)
        mean = sb("mean", [P, TILES], F32)
        rstd = sb("rstd", [P, TILES], F32)
        ln_a = sb("ln_a", [P, TILES], F32)
        ln_b = sb("ln_b", [P, TILES], F32)
        ln_d = sb("ln_d", [P, TILES], F32)
        ln_c = sb("ln_c", [P, TILES], F32)
        eps = sb("eps", [P, 1], F32)
        xn = sb("xn", [P, BT, DIM], F32)
        xT = sb("xT", [P, 2, BLK], F32)
        wi = sb("wi", [P, 3, HID], I32)
        w_gate = sb("w_gate", [P, HID], F32)
        w_up = sb("w_up", [P, HID], F32)
        w_down = sb("w_down", [P, CH, DIM], F32)
        w_qkv = sb("w_qkv", [P, 3 * DIM], F32)
        w_out = sb("w_out", [P, DIM], F32)
        b_qk = sb("b_qk", [P, 2], F32)
        b_v = sb("b_v", [P, DIM], F32)
        b_out = sb("b_out", [P, DIM], F32)
        ident = sb("ident", [P, P], F32)
        ident_b = sb("ident_b", [P, P], BF16)
        silu = sb("silu", [P, CH, BLK], F32)
        hid = sb("hid", [P, 2, CH, BLK], F32)
        parts = sb("parts", [P, 2, 2, PARTS, BLK], BF16)
        resid = sb("resid", [P, 2, 2, BLK], F32)
        v_all = sb("v_all", [P, PAIRS, KT, 2 * DH], F32)
        v_stage = sb("v_stage", [P, NBUF, KT, 2, VW], F32)
        q_stack = sb("q_stack", [P, NBUF, 2, SEQ], BF16)
        k_stack = sb("k_stack", [P, NBUF, 2, SEQ], BF16)
        probs = sb("probs", [P, 2, 4, UQ], F32)
        nmax = sb("nmax", [P, 2, 2, BT], F32)
        zero = sb("zero", [P, 1], F32)
        m_res = sb("m_res", [P, 2, BT], F32)
        m_parts = sb("m_parts", [P, 2, 2, PARTS, BT], BF16)
        m_rows = sb("m_rows", [2 * PARTS * BT, 2, P], BF16)
        o_sb = sb("o_sb", [P, 256], F32)
        o_inv = sb("o_inv", [P, 2, 4], F32)
        att = sb("att", [P, PAIRS, KT, 2 * DH], F32)
        att_stage = sb("att_stage", [P, 2, BT, DIM], F32)
        attT = sb("attT", [P, 2, BLK], F32)

        ps_a = [psum(f"ps_a{h}", [P, 2, 512]) for h in range(2)]
        ps_b = [psum(f"ps_b{h}", [P, 512]) for h in range(2)]
        ps_o = psum("ps_o", [P, 512])
        ps_m = psum("ps_m", [P, 512])
        gate_bank = [ps_a[0][:, 0, :], ps_a[1][:, 0, :], ps_b[0][:, :]]
        up_bank = [ps_a[0][:, 1, :], ps_a[1][:, 1, :], ps_b[1][:, :]]
        q_bank = [ps_a[0][:, 0, :], ps_a[0][:, 1, :]]
        k_bank = [ps_a[1][:, 0, :], ps_a[1][:, 1, :]]
        v_bank = [ps_b[0][:, :], ps_b[1][:, :]]
        m_psum = ps_m[:, 256:512].bitcast(BF16)[0:2 * PARTS * BT, 0:P]
        o_psum = ps_m[:, 0:256].rearrange("p (b h q c) -> p b h q c", b=2, h=2, q=2)

        x_loaded = sem("x_loaded")
        w_loaded = sem("w_loaded")
        consts_set = sem("consts_set")
        zeroed = sem("zeroed")
        weights_ready = sem("weights_ready")
        stats_done = sem("stats_done")
        ln_chain = sem("ln_chain")
        var_ready = sem("var_ready")
        std_ready = sem("std_ready")
        ln_ready = sem("ln_ready")
        xn_ready = sem("xn_ready")
        xT_done = sem("xT_done")
        xT_copied = sem("xT_copied")
        gate_done = sem("gate_done")
        up_done = sem("up_done")
        silu_done = sem("silu_done")
        hid_done = sem("hid_done")
        down_done = sem("down_done")
        res_done = sem("res_done")
        q_done = sem("q_done")
        k_done = sem("k_done")
        v_done = sem("v_done")
        v_added = sem("v_added")
        hi_done = sem("hi_done")
        resid_done = sem("resid_done")
        q_mid_done = sem("q_mid_done")
        k_mid_done = sem("k_mid_done")
        q_low_done = sem("q_low_done")
        k_low_done = sem("k_low_done")
        stored = [sem(f"stored{i}") for i in range(2)]
        qk_loaded = [sem(f"qk_loaded{i}") for i in range(NBUF)]
        v_staged = sem("v_staged")
        a_ready = sem("a_ready")
        max_done = sem("max_done")
        split_chain = sem("split_chain")
        m_split = sem("m_split")
        misc_ready = sem("misc_ready")
        misc_read = sem("misc_read")
        m_rows_ready = sem("m_rows_ready")
        m_loaded = [sem(f"m_loaded{i}") for i in range(2)]
        s_ready = sem("s_ready")
        exp_done = sem("exp_done")
        pv_done = sem("pv_done")
        o_copied = sem("o_copied")
        inv_done = sem("inv_done")
        att_written = sem("att_written")
        bias_added = sem("bias_added")
        staged = sem("staged")
        attT_done = sem("attT_done")
        attT_copied = sem("attT_copied")
        proj_done = sem("proj_done")
        proj_added = sem("proj_added")
        out_stored = sem("out_stored")

        block = ctx.enter_context(nc.Block())

        @block.sync
        def _(sp):
            x_t = x_in.rearrange("(t p) d -> p t d", p=P)
            for b in range(BATCH):
                sp.dma_start(x[:, KT * b:KT * (b + 1), :], x_t[:, KT * b:KT * (b + 1), :]).then_inc(x_loaded, 16)

            def store(n, par, b):
                for t, scr, ready in ((0, q_scr, q_low_done), (1, k_scr, k_low_done)):
                    sp.wait_ge(ready, n + 1)
                    for i in range(PARTS):
                        dst = scr[bass.ds(HP * b, HP), i].rearrange("hp h d t -> hp (h d) t")
                        sp.dma_start(dst[:, :, par * BLK:(par + 1) * BLK],
                                     parts[:, par, t, i, :]).then_inc(stored[par], 16)

            run_blocks(sp, store)
            for par in range(2):
                sp.wait_ge(stored[par], 16 * 2 * PARTS * NBLK // 2)
            sp.wait_ge(zeroed, 1)

            def load_stacks(p, c):
                for h in range(2):
                    for i in range(PARTS):
                        lo = i * PARTS * DH
                        q_part = q_scr[bass.ds(p, 1), i, h].broadcast_to((PARTS, DH, SEQ))
                        sp.dma_start(q_stack[lo:lo + PARTS * DH, c, h, :], q_part).then_inc(qk_loaded[c], 16)
                        k_parts = k_scr[bass.ds(p, 1), :, h].rearrange("o i d t -> (o i) d t")
                        sp.dma_start(k_stack[lo:lo + PARTS * DH, c, h, :], k_parts).then_inc(qk_loaded[c], 16)

            def load_max(v, half, c):
                sp.wait_ge(m_rows_ready, v + 1)
                for h in range(2):
                    dst = q_stack[QK_ROWS:ALL_ROWS, c, h, half * UQ:(half + 1) * UQ]
                    lo = h * PARTS * BT
                    sp.dma_start(dst.rearrange("i (t q) -> i t q", t=BT),
                                 m_rows[lo:lo + PARTS * BT, half, :]).then_inc(m_loaded[half], 16)

            for p in range(NBUF):
                load_stacks(p, p)
            load_max(0, 0, 0)

            def pair(p, c, i):
                load_max(2 * p + 1, 1, c)
                if not (isinstance(p, int) and p == PAIRS - 1):
                    load_max(2 * p + 2, 0, (c + 1) % NBUF)
                if not (isinstance(p, int) and p + NBUF >= PAIRS):
                    sp.wait_ge(s_ready, 4 * STEPS * 2 * (p + 1))
                    load_stacks(p + NBUF, c)

            run_pairs(sp, pair, 1)

            out_t = out.rearrange("(t p) d -> p t d", p=P)

            def write(n, par, b):
                sp.wait_ge(res_done, NBLK + n + 1)
                sp.dma_start(out_t[:, bass.ds(BT * n, BT), :],
                             x[:, bass.ds(BT * n, BT), :]).then_inc(out_stored, 16)

            run_blocks(sp, write)
            sp.wait_ge(out_stored, 16 * NBLK)

        @block.gpsimd
        def _(pool):
            pool.memset(ident[:], 0.0).then_inc(split_chain, 1)
            pool.memset(ident_b[:], 0.0).then_inc(split_chain, 1)
            pool.wait_ge(split_chain, 2)
            pool.affine_select(out=ident[:], in_=ident[:], compare_op=ALU.not_equal, fill=1.0, base=0,
                               pattern=[[-1, P]], channel_multiplier=1)
            pool.affine_select(out=ident_b[:], in_=ident_b[:], compare_op=ALU.not_equal, fill=1.0, base=0,
                               pattern=[[-1, P]], channel_multiplier=1).then_inc(consts_set, 1)
            pool.memset(v_stage[:], 0.0).then_inc(split_chain, 1)
            pool.wait_ge(split_chain, 3)
            pool.memset(v_stage[:, :, :, :, DH:DH + 1], 1.0)
            pool.memset(q_stack[:], 0.0)
            pool.memset(zero[:, :], 0.0)
            pool.memset(k_stack[:], 1.0).then_inc(zeroed, 1)

            def split_block(n, par, b):
                pool.wait_ge(resid_done, 2 * n + 2)
                pool.tensor_tensor(parts[:, par, 1, 1, :], resid[:, par, 1, :],
                                   zero[:, :].broadcast_to((P, BLK)), ALU.add).then_inc(k_mid_done, 1)
                pool.wait_ge(k_mid_done, n + 1)
                pool.tensor_tensor(parts[:, par, 1, 2, :], resid[:, par, 1, :], parts[:, par, 1, 1, :],
                                   ALU.subtract).then_inc(k_low_done, 1)

            pool.wait_ge(zeroed, 1)
            run_blocks(pool, split_block)

            def stage_v(p, c):
                if past(p - NBUF + 1):
                    pool.wait_ge(pv_done, 2 * STEPS * (p - NBUF + 1))
                pool.tensor_tensor(v_stage[:, c, :, :, 0:DH],
                                   v_all[:, bass.ds(p, 1), :, :].rearrange("p o k (h d) -> p (o k) h d", h=2),
                                   zero[:, :].unsqueeze(2).unsqueeze(3).broadcast_to((P, KT, 2, DH)),
                                   ALU.add).then_inc(v_staged, 1)

            def split_max(v, half):
                m, hi, mid, low = (nmax[:, half], m_parts[:, half, :, 0, :], m_parts[:, half, :, 1, :],
                                   m_parts[:, half, :, 2, :])
                pool.wait_ge(max_done, 2 * BT * (v + 1))
                if past(v - 1):
                    pool.wait_ge(misc_ready, v - 1)
                z = zero[:, :].unsqueeze(2).broadcast_to((P, 2, BT))
                pool.tensor_tensor(hi, m, z, ALU.add).then_inc(split_chain, 1)
                pool.wait_ge(split_chain, 3 * v + 4)
                pool.tensor_tensor(m_res[:], m, hi, ALU.subtract).then_inc(split_chain, 1)
                pool.wait_ge(split_chain, 3 * v + 5)
                pool.tensor_tensor(mid, m_res[:], z, ALU.add).then_inc(split_chain, 1)
                pool.wait_ge(split_chain, 3 * v + 6)
                pool.tensor_tensor(low, m_res[:], mid, ALU.subtract).then_inc(m_split, 1)

            pool.wait_ge(v_added, NBLK)
            stage_v(0, 0)
            split_max(0, 0)

            def pair(p, c, i):
                last = isinstance(p, int) and p == PAIRS - 1
                if not last:
                    stage_v(p + 1, (c + 1) % NBUF)
                split_max(2 * p + 1, 1)
                if not last:
                    split_max(2 * p + 2, 0)

            pool.wait_ge(xn_ready, 2 * NBLK)
            pool.wait_ge(w_loaded, 16 * 9)
            pool.tensor_tensor(x[:], x[:], b_out[:, :].unsqueeze(1).broadcast_to((P, TILES, DIM)),
                               ALU.add).then_inc(bias_added, 1)
            run_pairs(pool, pair, 4)

        @block.scalar
        def _(act):
            act.dma_start(wi[:, 0, :], wg_t).then_inc(w_loaded, 16)
            act.dma_start(wi[:, 1, :], wu_t).then_inc(w_loaded, 16)
            act.dma_start(wi[:, 2, :].rearrange("p (c d) -> p c d", c=CH),
                          wd_t.rearrange("(c p) d -> p c d", p=P)).then_inc(w_loaded, 16)
            act.dma_start(w_qkv[:, :], wqkv_t).then_inc(w_loaded, 16)
            act.dma_start(w_out[:, :], wo_t).then_inc(w_loaded, 16)
            for t in range(2):
                act.dma_start(b_qk[:, t:t + 1],
                              qkv_b[t * DIM:(t + 1) * DIM].rearrange("(p o) -> p o", o=1)).then_inc(w_loaded, 16)
            act.dma_start(b_v[:, :], qkv_b[2 * DIM:3 * DIM].rearrange("(o d) -> o d", o=1)
                          .broadcast_to((P, DIM))).then_inc(w_loaded, 16)
            act.dma_start(b_out[:, :], out_b.rearrange("(o d) -> o d", o=1)
                          .broadcast_to((P, DIM))).then_inc(w_loaded, 16)

            def std(k):
                act.wait_ge(var_ready, k + 1)
                act.activation(rstd[:, :], ln_a[:, :], ACT.Sqrt, bias=eps[:, 0:1]).then_inc(std_ready, 1)

            def copy_xT(L, par):
                act.wait_ge(xT_done, L + 1)
                act.copy(xT[:, par, :], ps_m[:, :]).then_inc(xT_copied, 1)

            def ffn(f0, l0):
                def step(n, par, b):
                    f = f0 + n
                    for c in range(CH):
                        act.wait_ge(gate_done, CH * f + c + 1)
                        if past(CH * f + c + 1 - CH):
                            act.wait_ge(hid_done, CH * f + c + 1 - CH)
                        act.activation(silu[:, c, :], gate_bank[c], ACT.Silu).then_inc(silu_done, 1)
                    if not (isinstance(n, int) and n == NBLK - 1):
                        copy_xT(l0 + n + 1, 1 - par)

                copy_xT(l0, 0)
                run_blocks(act, step)

            std(0)
            ffn(0, 0)
            std(1)

            def qkv_step(n, par, b):
                if past(b):
                    act.wait_ge(stored[par], 16 * 2 * PARTS * b)
                for t, bank, done in ((0, q_bank[par], q_done), (1, k_bank[par], k_done)):
                    act.wait_ge(done, n + 1)
                    act.activation(parts[:, par, t, 0, :], bank, ACT.Identity,
                                   bias=b_qk[:, t:t + 1]).then_inc(hi_done, 1)
                if not (isinstance(n, int) and n == NBLK - 1):
                    copy_xT(NBLK + n + 1, 1 - par)

            copy_xT(NBLK, 0)
            run_blocks(act, qkv_step)

            def unit(u, p, c, half):
                for s in range(STEPS):
                    g = STEPS * u + s
                    for i in range(4):
                        act.wait_ge(s_ready, 4 * g + i + 1)
                        if i == 0 and past(g - 1):
                            act.wait_ge(pv_done, g - 1)
                        act.activation(probs[:, s % 2, i, :], ps_b[i % 2][:, :], ACT.Exp,
                                       scale=SCALE_QK).then_inc(exp_done, 1)
                        if s == 0 and i == 2 and past(u):
                            copy_o(u - 1)

            def copy_o(u):
                act.wait_ge(pv_done, STEPS * (u + 1))
                act.wait_ge(misc_ready, u + 1)
                act.copy(o_sb[:, :], ps_o[:, 0:256]).then_inc(o_copied, 1)

            def first_pair(p, c, i):
                unit(2 * p, p, c, 0)
                unit(2 * p + 1, p, c, 1)

            unit(0, 0, 0, 0)
            unit(1, 0, 0, 1)
            with act.Fori(1, PAIRS) as p:
                first_pair(p, 0, 0)
            copy_o(2 * PAIRS - 1)

            def proj_step(n, par, b):
                if past(n - 1):
                    act.wait_ge(attT_done, n - 1)
                act.copy(att_stage[:, par, :, :].rearrange("p t (hp e) -> p t hp e", hp=HP),
                         att[:, bass.ds(HP * b, HP), par * BT:(par + 1) * BT, :]
                         .rearrange("p hp t e -> p t hp e")).then_inc(staged, 1)
                act.wait_ge(attT_done, n + 1)
                act.copy(attT[:, par, :], ps_m[:, :]).then_inc(attT_copied, 1)

            act.wait_ge(att_written, 2 * PAIRS)
            run_blocks(act, proj_step)
            std(2)
            ffn(NBLK, 2 * NBLK)

        @block.vector
        def _(dve):
            dve.memset(eps[:, :], EPS).then_inc(consts_set, 1)
            dve.wait_ge(w_loaded, 16 * 9)
            dve.tensor_scalar(w_gate[:, :], wi[:, 0, :], SCALE_INT8, None, ALU.mult)
            dve.tensor_scalar(w_up[:, :], wi[:, 1, :], SCALE_INT8, None, ALU.mult)
            dve.tensor_scalar(w_down[:, :, :].rearrange("p c d -> p (c d)"), wi[:, 2, :], SCALE_INT8, None,
                              ALU.mult).then_inc(weights_ready, 1)

            chain = [0]

            def link(ins):
                chain[0] += 1
                ins.then_inc(ln_chain, 1)
                dve.wait_ge(ln_chain, chain[0])

            def finish_stats(k):
                mean_e, ss_e, mean_o, ss_o = stats[:, :, 1], stats[:, :, 2], stats[:, :, 4], stats[:, :, 5]
                link(dve.tensor_tensor(ln_a[:, :], mean_e, mean_o, ALU.subtract))
                link(dve.scalar_tensor_tensor(ln_b[:, :], ln_a[:, :], 0.25, ln_a[:, :], ALU.mult, ALU.mult))
                link(dve.tensor_tensor(ln_c[:, :], ss_e, ss_o, ALU.add))
                dve.scalar_tensor_tensor(ln_a[:, :], ln_c[:, :], 1.0 / DIM, ln_b[:, :], ALU.mult,
                                         ALU.add).then_inc(var_ready, 1)
                link(dve.tensor_tensor(ln_d[:, :], mean_e, mean_o, ALU.add))
                link(dve.tensor_scalar(mean[:, :], ln_d[:, :], 0.5, None, ALU.mult))
                dve.wait_ge(std_ready, k + 1)
                link(dve.reciprocal(rstd[:, :], rstd[:, :]))

            def norm(n, L):
                if past(L):
                    dve.wait_ge(xT_done, L)
                for j in range(BT):
                    t = BT * n + j
                    ins = dve.tensor_scalar(xn[:, j, :],
                                            x[:, bass.ds(t, 1), :].rearrange("p o d -> p (o d)"),
                                            mean[:, bass.ds(t, 1)], rstd[:, bass.ds(t, 1)],
                                            ALU.subtract, ALU.mult)
                ins.then_inc(xn_ready, 1)

            def block_stats(n):
                for j in range(BT):
                    t = BT * n + j
                    ins = dve.bn_stats(stats[:, bass.ds(t, 1), :].rearrange("p o s -> p (o s)"),
                                       x[:, bass.ds(t, 1), :].rearrange("p o d -> p (o d)"))
                return ins

            def ffn(f0, l0, with_stats):
                def residual(n):
                    f = f0 + n
                    rows = x[:, bass.ds(BT * n, BT), :].rearrange("p t d -> p (t d)")
                    dve.wait_ge(down_done, f + 1)
                    dve.scalar_tensor_tensor(rows, ps_o[:, :], 0.5, rows, ALU.mult, ALU.add).then_inc(res_done, 1)
                    if with_stats:
                        dve.wait_ge(res_done, f + 1)
                        block_stats(n).then_inc(stats_done, 1)

                def step(n, par, b):
                    f = f0 + n
                    if not (isinstance(n, int) and n == NBLK - 1):
                        norm(n + 1, l0 + n + 1)
                    for c in range(CH):
                        dve.wait_ge(silu_done, CH * f + c + 1)
                        dve.wait_ge(up_done, CH * f + c + 1)
                        dve.tensor_tensor(hid[:, par, c, :], up_bank[c], silu[:, c, :],
                                          ALU.mult).then_inc(hid_done, 1)
                        if c == 0 and past(n):
                            residual(n - 1)

                norm(0, l0)
                run_blocks(dve, step)
                residual(NBLK - 1)

            for b in range(BATCH):
                dve.wait_ge(x_loaded, 16 * BATCH)
                for j in range(2):
                    ins = block_stats(2 * b + j)
            ins.then_inc(stats_done, 1)
            dve.wait_ge(stats_done, 1)
            finish_stats(0)
            ffn(0, 0, True)
            dve.wait_ge(stats_done, 1 + NBLK)
            finish_stats(1)

            def qkv_step(n, par, b):
                if not (isinstance(n, int) and n == NBLK - 1):
                    norm(n + 1, NBLK + n + 1)
                for t, bank in ((0, q_bank[par]), (1, k_bank[par])):
                    dve.wait_ge(hi_done, 2 * n + t + 1)
                    if t == 1 and past(n - 1):
                        dve.wait_ge(k_low_done, n - 1)
                    dve.scalar_tensor_tensor(resid[:, par, t, :], bank, b_qk[:, t:t + 1],
                                             parts[:, par, t, 0, :], ALU.add,
                                             ALU.subtract).then_inc(resid_done, 1)
                dve.wait_ge(v_done, n + 1)
                v_dst = v_all[:, bass.ds(HP * b, HP), par * BT:(par + 1) * BT, :].rearrange("p hp t e -> p t hp e")
                dve.tensor_tensor(v_dst, v_bank[par].rearrange("p (t hp e) -> p t hp e", t=BT, hp=HP),
                                  b_v[:, :].rearrange("p (hp e) -> p hp e", hp=HP).unsqueeze(1)
                                  .broadcast_to((P, BT, HP, 2 * DH)), ALU.add).then_inc(v_added, 1)
                dve.wait_ge(resid_done, 2 * n + 1)
                dve.tensor_copy(parts[:, par, 0, 1, :], resid[:, par, 0, :]).then_inc(q_mid_done, 1)
                dve.wait_ge(q_mid_done, n + 1)
                dve.tensor_tensor(parts[:, par, 0, 2, :], resid[:, par, 0, :], parts[:, par, 0, 1, :],
                                  ALU.subtract).then_inc(q_low_done, 1)

            norm(0, NBLK)
            run_blocks(dve, qkv_step)

            def maxima(v, half, s):
                if s == 0 and past(v - 1):
                    dve.wait_ge(m_split, v - 1)
                for h in range(2):
                    dve.wait_ge(a_ready, 2 * BT * v + 2 * s + h + 1)
                    dve.tensor_reduce(nmax[:, half, h, s:s + 1], ps_a[h][:, :, :], AX.XY, ALU.max,
                                      negate=True).then_inc(max_done, 1)

            def shared_round(r, v, v_half, w, w_pair, w_half):
                dve.wait_ge(misc_ready, r + 1)
                if v is not None:
                    if past(v - 1):
                        dve.wait_ge(m_loaded[v_half], 16 * 2 * v_pair(v, v_half))
                    ins = dve.tensor_copy(m_rows[:, v_half, :], m_psum)
                    ins.then_inc(m_rows_ready, 1)
                if w is None:
                    dve.wait_ge(m_rows_ready, v + 1)
                    dve.sem_inc(misc_read, 1)
                    return
                dve.reciprocal(o_inv[:, :, :].rearrange("p b (h q) -> p b h q", h=2),
                               o_psum[:, :, :, :, DH]).then_inc(inv_done, 1)
                dve.wait_ge(inv_done, w + 1)
                for h in range(2):
                    dst = att[:, bass.ds(w_pair, 1), w_half * BT:(w_half + 1) * BT, h * DH:(h + 1) * DH]
                    ins = dve.tensor_tensor(
                        dst.rearrange("p o (q b) e -> p b (o q) e", b=2), o_psum[:, :, h, :, 0:DH],
                        o_inv[:, :, 2 * h:2 * h + 2].unsqueeze(3).broadcast_to((P, 2, 2, DH)), ALU.mult)
                    if h == 1:
                        ins.then_inc(misc_read, 1)

            def v_pair(v, v_half):
                return v // 2 if isinstance(v, int) else v_pairs[0]

            v_pairs = [None]

            for s in range(STEPS):
                maxima(0, 0, s)
            maxima(1, 1, 0)
            maxima(1, 1, 1)
            shared_round(0, 0, 0, None, None, None)
            maxima(1, 1, 2)
            maxima(1, 1, 3)

            def pair(p, c, i):
                last = isinstance(p, int) and p == PAIRS - 1
                first = isinstance(p, int) and p == 0
                for half in range(2):
                    u = 2 * p + half
                    for s in range(STEPS):
                        if not last:
                            maxima(u + 2, half, s)
                        if s == 1:
                            v_pairs[0] = p if half == 0 else p + 1
                            v = None if last and half == 1 else u + 1
                            w = None if first and half == 0 else u - 1
                            shared_round(u + 1, v, 1 - half, w, p if half == 1 else p - 1, 1 - half)

            pair(0, 0, 0)
            with dve.Fori(1, PAIRS - 1) as p:
                pair(p, 0, 0)
            pair(PAIRS - 1, 0, 0)
            shared_round(2 * PAIRS + 1, None, None, 2 * PAIRS - 1, PAIRS - 1, 1)
            dve.wait_ge(misc_read, 2 * PAIRS + 2)
            dve.sem_inc(att_written, 2 * PAIRS)

            def proj_step(n, par, b):
                rows = x[:, bass.ds(BT * n, BT), :].rearrange("p t d -> p (t d)")
                dve.wait_ge(proj_done, n + 1)
                dve.tensor_tensor(rows, ps_o[:, :], rows, ALU.add).then_inc(proj_added, 1)
                dve.wait_ge(proj_added, n + 1)
                block_stats(n).then_inc(stats_done, 1)

            dve.wait_ge(bias_added, 1)
            run_blocks(dve, proj_step)
            dve.wait_ge(stats_done, 1 + 2 * NBLK)
            finish_stats(2)
            ffn(NBLK, 2 * NBLK, False)

        @block.tensor
        def _(pe):
            def transpose_xn(L):
                pe.wait_ge(xn_ready, L + 1)
                if past(L):
                    pe.wait_ge(xT_copied, L)
                for j in range(BT):
                    mm = pe.transpose(ps_m[:, j * P:(j + 1) * P], xn[:, j, :], ident[:, :])
                mm.then_inc(xT_done, 1)

            def ffn(f0, l0):
                def hidden(n, par, c):
                    f = f0 + n
                    free = CH * f + c + 1 - CH
                    if c == 0:
                        pe.wait_ge(xT_copied, l0 + n + 1)
                    if past(free):
                        pe.wait_ge(silu_done, free)
                    pe.matmul(gate_bank[c], w_gate[:, c * P:(c + 1) * P], xT[:, par, :],
                              start=True, stop=True).then_inc(gate_done, 1)
                    if past(free):
                        pe.wait_ge(hid_done, free)
                    pe.matmul(up_bank[c], w_up[:, c * P:(c + 1) * P], xT[:, par, :],
                              start=True, stop=True).then_inc(up_done, 1)

                def down(n, par):
                    f = f0 + n
                    pe.wait_ge(hid_done, CH * (f + 1))
                    if past(f):
                        pe.wait_ge(res_done, f)
                    for j in range(BT):
                        for c in range(CH):
                            mm = pe.matmul(ps_o[:, j * P:(j + 1) * P], hid[:, par, c, j * P:(j + 1) * P],
                                           w_down[:, c, :], start=(c == 0), stop=(c == CH - 1))
                    mm.then_inc(down_done, 1)

                def step(n, par, b):
                    hidden(n, par, 0)
                    if past(n):
                        down(n - 1, 1 - par)
                    hidden(n, par, 1)
                    hidden(n, par, 2)
                    if not (isinstance(n, int) and n == NBLK - 1):
                        transpose_xn(l0 + n + 1)

                transpose_xn(l0)
                run_blocks(pe, step)
                down(NBLK - 1, 1)

            pe.wait_ge(consts_set, 2)
            pe.wait_ge(weights_ready, 1)
            ffn(0, 0)

            def qkv_step(n, par, b):
                pe.wait_ge(xT_copied, NBLK + n + 1)
                if past(n - 1):
                    pe.wait_ge(resid_done, 2 * (n - 1))
                pe.matmul(q_bank[par], w_qkv[:, 0:DIM], xT[:, par, :], start=True, stop=True).then_inc(q_done, 1)
                pe.matmul(k_bank[par], w_qkv[:, DIM:2 * DIM], xT[:, par, :],
                          start=True, stop=True).then_inc(k_done, 1)
                if not (isinstance(n, int) and n == NBLK - 1):
                    transpose_xn(NBLK + n + 1)
                if past(n - 1):
                    pe.wait_ge(v_added, n - 1)
                for j in range(BT):
                    mm = pe.matmul(v_bank[par][:, j * P:(j + 1) * P], xT[:, par, j * P:(j + 1) * P],
                                   w_qkv[:, 2 * DIM:3 * DIM], start=True, stop=True)
                mm.then_inc(v_done, 1)

            transpose_xn(NBLK)
            pe.wait_ge(res_done, NBLK)
            run_blocks(pe, qkv_step)

            def scores_a(v, c, half, s, h, kh):
                q0 = half * UQ + s * P
                index = 2 * BT * v + 2 * s + h
                if kh == 0 and past(index - 1):
                    pe.wait_ge(max_done, index - 1)
                mm = pe.matmul(ps_a[h][:, kh, :], q_stack[0:QK_ROWS, c, h, q0:q0 + P],
                               k_stack[0:QK_ROWS, c, h, kh * 512:(kh + 1) * 512], start=True, stop=True)
                if kh == 1:
                    mm.then_inc(a_ready, 1)

            def scores_b(u, c, half, s, i):
                kt, h = 2 * s + i // 2, i % 2
                index = 4 * (STEPS * u + s) + i
                if past(index - 1):
                    pe.wait_ge(exp_done, index - 1)
                pe.matmul(ps_b[h][:, :], k_stack[0:ALL_ROWS, c, h, kt * P:(kt + 1) * P],
                          q_stack[0:ALL_ROWS, c, h, half * UQ:(half + 1) * UQ],
                          start=True, stop=True).then_inc(s_ready, 1)

            def pv(u, p, c, s):
                pe.wait_ge(exp_done, 4 * (STEPS * u + s + 1))
                if s == 0:
                    pe.wait_ge(v_staged, p + 1)
                    if past(u):
                        pe.wait_ge(o_copied, u)
                for k in range(2):
                    kt = 2 * s + k
                    for h in range(2):
                        for q in range(2):
                            j = 2 * h + q
                            mm = pe.matmul(ps_o[VW * j:VW * (j + 1), 0:256], v_stage[:, c, kt, h, :],
                                           probs[:, s % 2, 2 * k + h, q * 256:(q + 1) * 256],
                                           start=(kt == 0), stop=(kt == KT - 1))
                mm.then_inc(pv_done, 1)

            def shared_round(r, v, v_half, w):
                if past(r):
                    pe.wait_ge(misc_read, r)
                if w is not None:
                    pe.wait_ge(o_copied, w + 1)
                    for b in range(2):
                        mm = pe.transpose(ps_m[:, b * P:(b + 1) * P], o_sb[:, b * P:(b + 1) * P], ident[:, :])
                if v is not None:
                    pe.wait_ge(m_split, v + 1)
                    mm = pe.transpose(m_psum, m_parts[:, v_half].rearrange("p h i t -> p (h i t)"), ident_b[:, :])
                mm.then_inc(misc_ready, 1)

            pe.wait_ge(v_added, NBLK)
            pe.wait_ge(resid_done, 2 * NBLK)
            for v in range(2):
                if v == 0:
                    pe.wait_ge(qk_loaded[0], 16 * LOADS)
                for s in range(STEPS):
                    if v == 1 and s == 2:
                        shared_round(0, 0, 0, None)
                    for h in range(2):
                        for kh in range(2):
                            scores_a(v, 0, v, s, h, kh)

            def pair(p, c, i):
                last = isinstance(p, int) and p == PAIRS - 1
                first = isinstance(p, int) and p == 0
                nxt = (c + 1) % NBUF
                for half in range(2):
                    u = 2 * p + half
                    pe.wait_ge(m_loaded[half], 16 * 2 * (p + 1))
                    if half == 0 and not last:
                        pe.wait_ge(qk_loaded[nxt], 16 * LOADS * (i + (1 if c < NBUF - 1 else 2)))
                    for s in range(STEPS):
                        for h in range(2):
                            for k in range(2):
                                if not last:
                                    scores_a(u + 2, nxt, half, s, h, k)
                                scores_b(u, c, half, s, 2 * h + k)
                            if h == 0:
                                if s > 0:
                                    pv(u, p, c, s - 1)
                                elif half == 1:
                                    pv(u - 1, p, c, STEPS - 1)
                                elif not first:
                                    pv(u - 1, p - 1, (c - 1) % NBUF, STEPS - 1)
                        if s == 1:
                            shared_round(u + 1, None if last and half == 1 else u + 1, 1 - half,
                                         None if first and half == 0 else u - 1)

            run_pairs(pe, pair, 4)
            pv(2 * PAIRS - 1, PAIRS - 1, (PAIRS - 1) % NBUF, STEPS - 1)
            shared_round(2 * PAIRS + 1, None, None, 2 * PAIRS - 1)

            pe.wait_ge(misc_read, 2 * PAIRS + 2)

            def proj_step(n, par, b):
                pe.wait_ge(staged, n + 1)
                if past(n):
                    pe.wait_ge(attT_copied, n)
                for j in range(BT):
                    mm = pe.transpose(ps_m[:, j * P:(j + 1) * P], att_stage[:, par, j, :], ident[:, :])
                mm.then_inc(attT_done, 1)
                pe.wait_ge(attT_copied, n + 1)
                if past(n):
                    pe.wait_ge(proj_added, n)
                for j in range(BT):
                    mm = pe.matmul(ps_o[:, j * P:(j + 1) * P], attT[:, par, j * P:(j + 1) * P], w_out[:, :],
                                   start=True, stop=True)
                mm.then_inc(proj_done, 1)

            run_blocks(pe, proj_step)
            ffn(NBLK, 2 * NBLK)


def kernel(L0_attn_x, L0_attn_qkv_w, L0_attn_qkv_b, L0_attn_out_w, L0_attn_out_b, L0_ffn_w_gate, L0_ffn_w_up,
           L0_ffn_w_down):
    import numpy as np
    import concourse.bacc as bacc
    from concourse.bass_utils import run_bass_kernel_spmd as run

    arrays = {
        "x_in": np.ascontiguousarray(L0_attn_x).reshape(ROWS, DIM),
        "wqkv_t": np.ascontiguousarray(np.asarray(L0_attn_qkv_w).T),
        "qkv_b": np.ascontiguousarray(L0_attn_qkv_b),
        "wo_t": np.ascontiguousarray(np.asarray(L0_attn_out_w).T),
        "out_b": np.ascontiguousarray(L0_attn_out_b),
        "wg_t": np.ascontiguousarray(np.asarray(L0_ffn_w_gate).T),
        "wu_t": np.ascontiguousarray(np.asarray(L0_ffn_w_up).T),
        "wd_t": np.ascontiguousarray(np.asarray(L0_ffn_w_down).T),
    }
    nc = bacc.Bacc("TRN2", target_bir_lowering=False, num_devices=1)
    args = [nc.dram_tensor(name, a.shape, mybir.dt.from_np(a.dtype), kind="ExternalInput").ap()
            for name, a in arrays.items()]
    out = nc.dram_tensor("out", (ROWS, DIM), F32, kind="ExternalOutput").ap()
    macaron(nc, *args, out)
    r = run(nc, [arrays], core_ids=[0])
    return r.results[0]["out"].reshape(BATCH, SEQ, DIM)
```

```python
from contextlib import ExitStack

import concourse.bass as bass
from concourse import mybir

ALU = mybir.AluOpType
ACT = mybir.ActivationFunctionType
AX = mybir.AxisListType
F32 = mybir.dt.float32
BF16 = mybir.dt.bfloat16
I32 = mybir.dt.int32

P = 128
BATCH, SEQ, DIM = 4, 1024, 128
HEADS = 16
DH = DIM // HEADS
HID = 384
SCALE_INT8 = 1.0 / 127.0
SCALE_QK = float(DH) ** -0.5
EPS = 1e-5

ROWS = BATCH * SEQ
TILES = ROWS // P
BLK = 512
BT = BLK // P
NBLK = ROWS // BLK
CH = HID // P
HP = HEADS // 2
PAIRS = BATCH * HP
UQ = 512
KT = SEQ // P
STEPS = KT // 2
PARTS = 3
QK_ROWS = PARTS * PARTS * DH
ALL_ROWS = QK_ROWS + PARTS
NBUF = 3
VW = 32
LOADS = 1 + PARTS


def past(count):
    return not isinstance(count, int) or count > 0


def run_blocks(eng, step, after_first=None, before_last=None):
    step(0, 0, 0)
    if after_first:
        after_first()
    step(1, 1, 0)
    with eng.Fori(1, NBLK // 2 - 1) as i:
        step(2 * i, 0, i)
        step(2 * i + 1, 1, i)
    if before_last:
        before_last()
    step(NBLK - 2, 0, NBLK // 2 - 1)
    step(NBLK - 1, 1, NBLK // 2 - 1)


def run_pairs(eng, step, head, turns=9):
    for p in range(head):
        step(p, p % NBUF, p // NBUF)
    with eng.Fori(0, turns) as i:
        for k in range(head, head + NBUF):
            step(i * NBUF + k, k % NBUF, i + k // NBUF)
    for p in range(head + turns * NBUF, PAIRS):
        step(p, p % NBUF, p // NBUF)


def macaron(nc, x_in, wqkv_t, qk_b, v_b, wo_t, out_b, wg_t, wu_t, wd_t, out):
    with ExitStack() as ctx:
        def sb(name, shape, dt):
            return ctx.enter_context(nc.sbuf_tensor(name, shape, dt))

        def psum(name, shape):
            return ctx.enter_context(nc.psum_tensor(name, shape, F32))

        def sem(name):
            return ctx.enter_context(nc.semaphore(name))

        q_scr = nc.dram_tensor("q_parts_scratch", [PAIRS, PARTS, DH, 2, SEQ], BF16).ap()
        k_scr = nc.dram_tensor("k_parts_scratch", [PAIRS, PARTS, DH, 2, SEQ], BF16).ap()

        x = sb("x", [P, TILES, DIM], F32)
        stats = sb("stats", [P, TILES, 6], F32)
        mean = sb("mean", [P, TILES], F32)
        rstd = sb("rstd", [P, TILES], F32)
        ln_a = sb("ln_a", [P, TILES], F32)
        ln_b = sb("ln_b", [P, TILES], F32)
        ln_d = sb("ln_d", [P, TILES], F32)
        ln_c = sb("ln_c", [P, TILES], F32)
        eps = sb("eps", [P, 1], F32)
        xn = sb("xn", [P, 2, BT, DIM], F32)
        xT = sb("xT", [P, 2, BLK], F32)
        wi = sb("wi", [P, 3, HID], I32)
        w_gate = sb("w_gate", [P, HID], F32)
        w_up = sb("w_up", [P, HID], F32)
        w_down = sb("w_down", [P, CH, DIM], F32)
        w_qkv = sb("w_qkv", [P, 3 * DIM], F32)
        w_out = sb("w_out", [P, DIM], F32)
        b_qk = sb("b_qk", [P, 2], F32)
        b_v = sb("b_v", [P, 1], F32)
        b_out = sb("b_out", [P, DIM], F32)
        ident = sb("ident", [P, P], F32)
        ident_b = sb("ident_b", [P, P], BF16)
        silu = sb("silu", [P, CH, BLK], F32)
        hid = sb("hid", [P, 2, CH, BLK], F32)
        parts = sb("parts", [P, 2, 2, PARTS, BLK], BF16)
        resid = sb("resid", [P, 2, 2, BLK], F32)
        v_all = sb("v_all", [P, PAIRS, KT, 2 * DH], F32)
        v_stage = sb("v_stage", [P, NBUF, KT, 2, VW], F32)
        q_stack = sb("q_stack", [P, NBUF, 2, SEQ], BF16)
        k_stack = sb("k_stack", [P, NBUF, 2, SEQ], BF16)
        probs = sb("probs", [P, 2, 4, UQ], F32)
        nmax = sb("nmax", [P, 2, 2, BT], F32)
        zero = sb("zero", [P, 1], F32)
        m_res = sb("m_res", [P, 2, BT], F32)
        m_parts = sb("m_parts", [P, 2, 2, PARTS, BT], BF16)
        m_rows = sb("m_rows", [2 * PARTS * BT, 2, P], BF16)
        o_sb = sb("o_sb", [P, 256], F32)
        o_inv = sb("o_inv", [P, 2, 4], F32)
        att = sb("att", [P, PAIRS, KT, 2 * DH], F32)
        att_stage = sb("att_stage", [P, 2, BT, DIM], F32)
        attT = sb("attT", [P, 2, BLK], F32)

        ps_a = [psum(f"ps_a{h}", [P, 2, 512]) for h in range(2)]
        ps_b = [psum(f"ps_b{h}", [P, 512]) for h in range(2)]
        ps_o = psum("ps_o", [P, 512])
        ps_m = psum("ps_m", [P, 512])
        gate_bank = [ps_a[0][:, 0, :], ps_a[1][:, 0, :], ps_b[0][:, :]]
        up_bank = [ps_a[0][:, 1, :], ps_a[1][:, 1, :], ps_b[1][:, :]]
        q_bank = [ps_a[0][:, 0, :], ps_a[0][:, 1, :]]
        k_bank = [ps_a[1][:, 0, :], ps_a[1][:, 1, :]]
        v_bank = [ps_b[0][:, :], ps_b[1][:, :]]
        m_psum = ps_m[:, 256:512].bitcast(BF16)[0:2 * PARTS * BT, 0:P]
        o_psum = ps_m[:, 0:256].rearrange("p (b h q c) -> p b h q c", b=2, h=2, q=2)

        x_loaded = [sem(f"x_loaded{i}") for i in range(2)]
        ffn_w_loaded = sem("ffn_w_loaded")
        attn_w_loaded = sem("attn_w_loaded")
        consts_set = sem("consts_set")
        zeroed = sem("zeroed")
        weights_ready = sem("weights_ready")
        stats_done = sem("stats_done")
        ln_chain = sem("ln_chain")
        var_ready = sem("var_ready")
        std_ready = sem("std_ready")
        xn_ready = sem("xn_ready")
        xT_done = sem("xT_done")
        xT_copied = sem("xT_copied")
        gate_done = sem("gate_done")
        up_done = sem("up_done")
        silu_done = sem("silu_done")
        hid_done = sem("hid_done")
        down_done = sem("down_done")
        res_done = sem("res_done")
        q_done = sem("q_done")
        k_done = sem("k_done")
        v_done = sem("v_done")
        v_copied = sem("v_copied")
        hi_done = sem("hi_done")
        resid_done = sem("resid_done")
        q_mid_done = sem("q_mid_done")
        k_mid_done = sem("k_mid_done")
        q_low_done = sem("q_low_done")
        k_low_done = sem("k_low_done")
        stored = [sem(f"stored{i}") for i in range(2)]
        qk_loaded = [sem(f"qk_loaded{i}") for i in range(NBUF)]
        v_staged = sem("v_staged")
        a_ready = sem("a_ready")
        max_done = sem("max_done")
        split_chain = sem("split_chain")
        m_split = sem("m_split")
        misc_ready = sem("misc_ready")
        misc_read = sem("misc_read")
        m_rows_ready = sem("m_rows_ready")
        m_loaded = [sem(f"m_loaded{i}") for i in range(2)]
        s_ready = sem("s_ready")
        exp_done = sem("exp_done")
        pv_done = sem("pv_done")
        o_copied = sem("o_copied")
        inv_done = sem("inv_done")
        bias_added = sem("bias_added")
        staged = sem("staged")
        attT_done = sem("attT_done")
        attT_copied = sem("attT_copied")
        proj_done = sem("proj_done")
        proj_added = sem("proj_added")
        out_stored = sem("out_stored")

        block = ctx.enter_context(nc.Block())

        @block.sync
        def _(sp):
            x_t = x_in.rearrange("(t p) d -> p t d", p=P)
            for b in range(BATCH):
                sp.dma_start(x[:, KT * b:KT * (b + 1), :],
                             x_t[:, KT * b:KT * (b + 1), :]).then_inc(x_loaded[min(b, 1)], 16)

            def store(n, par, b):
                for t, scr, ready in ((0, q_scr, q_low_done), (1, k_scr, k_low_done)):
                    sp.wait_ge(ready, n + 1)
                    for i in range(PARTS):
                        dst = scr[bass.ds(HP * b, HP), i].rearrange("hp d h t -> hp (d h) t")
                        sp.dma_start(dst[:, :, par * BLK:(par + 1) * BLK],
                                     parts[:, par, t, i, :]).then_inc(stored[par], 16)

            def load_stacks(p, c):
                k_parts = k_scr[bass.ds(p, 1)].rearrange("o i d h t -> o (i d) (h t)")
                sp.dma_start(k_stack[0:QK_ROWS, c, :, :],
                             k_parts.broadcast_to((PARTS, PARTS * DH, 2 * SEQ))).then_inc(qk_loaded[c], 16)
                for i in range(PARTS):
                    lo = i * PARTS * DH
                    q_part = q_scr[bass.ds(p, 1), i].rearrange("o d h t -> o d (h t)")
                    sp.dma_start(q_stack[lo:lo + PARTS * DH, c, :, :],
                                 q_part.broadcast_to((PARTS, DH, 2 * SEQ))).then_inc(qk_loaded[c], 16)

            def wait_stored(blocks):
                for par in range(2):
                    sp.wait_ge(stored[par], 16 * 2 * PARTS * blocks // 2)

            store(0, 0, 0)
            store(1, 1, 0)
            wait_stored(2)
            sp.wait_ge(zeroed, 1)
            load_stacks(0, 0)
            with sp.Fori(1, BATCH) as b:
                store(2 * b, 0, b)
                store(2 * b + 1, 1, b)
            wait_stored(NBLK)
            for p in range(1, NBUF):
                load_stacks(p, p)

            def load_max(v, half, c):
                sp.wait_ge(m_rows_ready, v + 1)
                for h in range(2):
                    dst = q_stack[QK_ROWS:ALL_ROWS, c, h, half * UQ:(half + 1) * UQ]
                    lo = h * PARTS * BT
                    sp.dma_start(dst.rearrange("i (t q) -> i t q", t=BT),
                                 m_rows[lo:lo + PARTS * BT, half, :]).then_inc(m_loaded[half], 16)

            load_max(0, 0, 0)

            def pair(p, c, i):
                load_max(2 * p + 1, 1, c)
                if not (isinstance(p, int) and p == PAIRS - 1):
                    load_max(2 * p + 2, 0, (c + 1) % NBUF)
                if not (isinstance(p, int) and p + NBUF >= PAIRS):
                    sp.wait_ge(s_ready, 4 * STEPS * 2 * (p + 1))
                    load_stacks(p + NBUF, c)

            run_pairs(sp, pair, 1)

            out_t = out.rearrange("(t p) d -> p t d", p=P)

            def write(n, par, b):
                sp.wait_ge(res_done, NBLK + n + 1)
                sp.dma_start(out_t[:, bass.ds(BT * n, BT), :],
                             x[:, bass.ds(BT * n, BT), :]).then_inc(out_stored, 16)

            run_blocks(sp, write)
            sp.wait_ge(out_stored, 16 * NBLK)

        @block.gpsimd
        def _(pool):
            pool.memset(ident[:], 0.0).then_inc(split_chain, 1)
            pool.memset(ident_b[:], 0.0).then_inc(split_chain, 1)
            pool.wait_ge(split_chain, 2)
            pool.affine_select(out=ident[:], in_=ident[:], compare_op=ALU.not_equal, fill=1.0, base=0,
                               pattern=[[-1, P]], channel_multiplier=1)
            pool.affine_select(out=ident_b[:], in_=ident_b[:], compare_op=ALU.not_equal, fill=1.0, base=0,
                               pattern=[[-1, P]], channel_multiplier=1).then_inc(consts_set, 1)
            pool.memset(v_stage[:], 0.0).then_inc(split_chain, 1)
            pool.wait_ge(split_chain, 3)
            pool.memset(v_stage[:, :, :, :, DH:DH + 1], 1.0)
            pool.memset(q_stack[:], 0.0)
            pool.memset(zero[:, :], 0.0)
            pool.memset(k_stack[:], 1.0).then_inc(zeroed, 1)

            def split_block(n, par, b):
                pool.wait_ge(resid_done, 2 * n + 2)
                pool.tensor_tensor(parts[:, par, 1, 1, :], resid[:, par, 1, :],
                                   zero[:, :].broadcast_to((P, BLK)), ALU.add).then_inc(k_mid_done, 1)
                pool.wait_ge(k_mid_done, n + 1)
                pool.tensor_tensor(parts[:, par, 1, 2, :], resid[:, par, 1, :], parts[:, par, 1, 1, :],
                                   ALU.subtract).then_inc(k_low_done, 1)

            pool.wait_ge(zeroed, 1)
            run_blocks(pool, split_block)

            def stage_v(p, c):
                if past(p - NBUF + 1):
                    pool.wait_ge(pv_done, 2 * STEPS * (p - NBUF + 1))
                pool.tensor_tensor(v_stage[:, c, :, :, 0:DH],
                                   v_all[:, bass.ds(p, 1), :, :].rearrange("p o k (h d) -> p (o k) h d", h=2),
                                   zero[:, :].unsqueeze(2).unsqueeze(3).broadcast_to((P, KT, 2, DH)),
                                   ALU.add).then_inc(v_staged, 1)

            def split_max(v, half):
                m, hi, mid, low = (nmax[:, half], m_parts[:, half, :, 0, :], m_parts[:, half, :, 1, :],
                                   m_parts[:, half, :, 2, :])
                pool.wait_ge(max_done, 2 * BT * (v + 1))
                if past(v - 1):
                    pool.wait_ge(misc_ready, v - 1)
                z = zero[:, :].unsqueeze(2).broadcast_to((P, 2, BT))
                pool.tensor_tensor(hi, m, z, ALU.add).then_inc(split_chain, 1)
                pool.wait_ge(split_chain, 3 * v + 4)
                pool.tensor_tensor(m_res[:], m, hi, ALU.subtract).then_inc(split_chain, 1)
                pool.wait_ge(split_chain, 3 * v + 5)
                pool.tensor_tensor(mid, m_res[:], z, ALU.add).then_inc(split_chain, 1)
                pool.wait_ge(split_chain, 3 * v + 6)
                pool.tensor_tensor(low, m_res[:], mid, ALU.subtract).then_inc(m_split, 1)

            pool.wait_ge(v_copied, NBLK)
            stage_v(0, 0)
            split_max(0, 0)

            def pair(p, c, i):
                last = isinstance(p, int) and p == PAIRS - 1
                if not last:
                    stage_v(p + 1, (c + 1) % NBUF)
                split_max(2 * p + 1, 1)
                if not last:
                    split_max(2 * p + 2, 0)

            pool.wait_ge(xn_ready, 2 * NBLK)
            pool.wait_ge(attn_w_loaded, 16 * 5)
            pool.tensor_tensor(x[:], x[:], b_out[:, :].unsqueeze(1).broadcast_to((P, TILES, DIM)),
                               ALU.add).then_inc(bias_added, 1)
            run_pairs(pool, pair, 4)

        @block.scalar
        def _(act):
            act.dma_start(wi[:, 0, :], wg_t).then_inc(ffn_w_loaded, 16)
            act.dma_start(wi[:, 1, :], wu_t).then_inc(ffn_w_loaded, 16)
            act.dma_start(wi[:, 2, :].rearrange("p (c d) -> p c d", c=CH),
                          wd_t.rearrange("(c p) d -> p c d", p=P)).then_inc(ffn_w_loaded, 16)

            def load_attention_weights():
                act.dma_start(w_qkv[:, :], wqkv_t).then_inc(attn_w_loaded, 16)
                act.dma_start(w_out[:, :], wo_t).then_inc(attn_w_loaded, 16)
                act.dma_start(b_qk[:, :], qk_b).then_inc(attn_w_loaded, 16)
                act.dma_start(b_v[:, :], v_b.rearrange("(p o) -> p o", o=1)).then_inc(attn_w_loaded, 16)
                act.dma_start(b_out[:, :], out_b.rearrange("(o d) -> o d", o=1)
                              .broadcast_to((P, DIM))).then_inc(attn_w_loaded, 16)

            def std(k, lo, hi):
                act.wait_ge(var_ready, k + 1)
                act.activation(rstd[:, lo:hi], ln_a[:, lo:hi], ACT.Sqrt, bias=eps[:, 0:1]).then_inc(std_ready, 1)

            def copy_xT(L, par):
                act.wait_ge(xT_done, L + 1)
                act.copy(xT[:, par, :], ps_m[:, :]).then_inc(xT_copied, 1)

            def ffn(f0, l0, after_first=None):
                def step(n, par, b):
                    f = f0 + n
                    for c in range(CH):
                        if c == CH - 1 and not (isinstance(n, int) and n == NBLK - 1):
                            copy_xT(l0 + n + 1, 1 - par)
                        act.wait_ge(gate_done, CH * f + c + 1)
                        if past(CH * f + c + 1 - CH):
                            act.wait_ge(hid_done, CH * f + c + 1 - CH)
                        act.activation(silu[:, c, :], gate_bank[c], ACT.Silu).then_inc(silu_done, 1)

                run_blocks(act, step, after_first)

            std(0, 0, KT)
            copy_xT(0, 0)
            load_attention_weights()
            ffn(0, 0, lambda: std(1, KT, TILES))
            std(2, 0, TILES - BT)
            copy_xT(NBLK, 0)
            std(3, TILES - BT, TILES)

            def qkv_step(n, par, b):
                if past(b):
                    act.wait_ge(stored[par], 16 * 2 * PARTS * b)
                for t, bank, done in ((0, q_bank[par], q_done), (1, k_bank[par], k_done)):
                    act.wait_ge(done, n + 1)
                    act.activation(parts[:, par, t, 0, :], bank, ACT.Identity,
                                   bias=b_qk[:, t:t + 1]).then_inc(hi_done, 1)
                if not (isinstance(n, int) and n == NBLK - 1):
                    copy_xT(NBLK + n + 1, 1 - par)
                v_dst = v_all[:, bass.ds(HP * b, HP), par * BT:(par + 1) * BT, :].rearrange("p hp t e -> p t hp e")
                act.wait_ge(v_done, n + 1)
                act.copy(v_dst, v_bank[par].rearrange("p (t hp e) -> p t hp e", t=BT, hp=HP)).then_inc(v_copied, 1)

            act.wait_ge(attn_w_loaded, 16 * 5)
            run_blocks(act, qkv_step)

            def unit(u, half):
                for s in range(STEPS):
                    g = STEPS * u + s
                    for i in range(4):
                        act.wait_ge(s_ready, 4 * g + i + 1)
                        if i == 0 and past(g - 1):
                            act.wait_ge(pv_done, g - 1)
                        act.activation(probs[:, s % 2, i, :], ps_b[i % 2][:, :], ACT.Exp,
                                       scale=SCALE_QK).then_inc(exp_done, 1)
                        if s == 0 and i == 2 and past(u):
                            copy_o(u - 1)

            def copy_o(u):
                act.wait_ge(pv_done, STEPS * (u + 1))
                act.wait_ge(misc_ready, u + 1)
                act.copy(o_sb[:, :], ps_o[:, 0:256]).then_inc(o_copied, 1)

            for half in range(2):
                unit(half, half)
            with act.Fori(1, PAIRS) as p:
                for half in range(2):
                    unit(2 * p + half, half)
            copy_o(2 * PAIRS - 1)

            def stage(n, par, b):
                if past(n - 1):
                    act.wait_ge(attT_done, n - 1)
                act.copy(att_stage[:, par, :, :].rearrange("p t (hp e) -> p t hp e", hp=HP),
                         att[:, bass.ds(HP * b, HP), par * BT:(par + 1) * BT, :]
                         .rearrange("p hp t e -> p t hp e")).then_inc(staged, 1)

            def proj_step(n, par, b):
                if not (isinstance(n, int) and n == NBLK - 1):
                    stage(n + 1, 1 - par, b + par)
                act.wait_ge(attT_done, n + 1)
                if past(n - 1):
                    act.wait_ge(proj_done, n - 1)
                act.activation(attT[:, par, :], ps_b[par][:, :], ACT.Identity,
                               bias=b_v[:, 0:1]).then_inc(attT_copied, 1)

            act.wait_ge(misc_read, 2 * PAIRS + 2)
            stage(0, 0, 0)
            run_blocks(act, proj_step, before_last=lambda: std(4, 0, TILES - 2 * BT))
            copy_xT(2 * NBLK, 0)
            std(5, TILES - 2 * BT, TILES)
            ffn(NBLK, 2 * NBLK)

        @block.vector
        def _(dve):
            dve.memset(eps[:, :], EPS).then_inc(consts_set, 1)
            chain = [0]

            def link(ins):
                chain[0] += 1
                ins.then_inc(ln_chain, 1)
                dve.wait_ge(ln_chain, chain[0])

            def variance(lo, hi):
                t = slice(lo, hi)
                mean_e, ss_e, mean_o, ss_o = stats[:, t, 1], stats[:, t, 2], stats[:, t, 4], stats[:, t, 5]
                dve.tensor_tensor(ln_c[:, t], ss_e, ss_o, ALU.add)
                dve.tensor_tensor(ln_d[:, t], mean_e, mean_o, ALU.add)
                link(dve.tensor_tensor(ln_a[:, t], mean_e, mean_o, ALU.subtract))
                dve.tensor_scalar(mean[:, t], ln_d[:, t], 0.5, None, ALU.mult)
                link(dve.scalar_tensor_tensor(ln_b[:, t], ln_a[:, t], 0.25, ln_a[:, t], ALU.mult, ALU.mult))
                dve.scalar_tensor_tensor(ln_a[:, t], ln_c[:, t], 1.0 / DIM, ln_b[:, t], ALU.mult,
                                         ALU.add).then_inc(var_ready, 1)

            def inverse(k, lo, hi):
                dve.wait_ge(std_ready, k + 1)
                link(dve.reciprocal(rstd[:, lo:hi], rstd[:, lo:hi]))

            def norm(n, L, par):
                if past(L - 1):
                    dve.wait_ge(xT_done, L - 1)
                for j in range(BT):
                    t = BT * n + j
                    ins = dve.tensor_scalar(xn[:, par, j, :],
                                            x[:, bass.ds(t, 1), :].rearrange("p o d -> p (o d)"),
                                            mean[:, bass.ds(t, 1)], rstd[:, bass.ds(t, 1)],
                                            ALU.subtract, ALU.mult)
                ins.then_inc(xn_ready, 1)

            def block_stats(n):
                for j in range(BT):
                    t = BT * n + j
                    ins = dve.bn_stats(stats[:, bass.ds(t, 1), :].rearrange("p o s -> p (o s)"),
                                       x[:, bass.ds(t, 1), :].rearrange("p o d -> p (o d)"))
                return ins

            def ffn(f0, l0, with_stats):
                def residual(n):
                    f = f0 + n
                    rows = x[:, bass.ds(BT * n, BT), :].rearrange("p t d -> p (t d)")
                    dve.wait_ge(down_done, f + 1)
                    dve.scalar_tensor_tensor(rows, ps_o[:, :], 0.5, rows, ALU.mult, ALU.add).then_inc(res_done, 1)
                    if with_stats:
                        dve.wait_ge(res_done, f + 1)
                        block_stats(n).then_inc(stats_done, 1)

                def step(n, par, b):
                    f = f0 + n
                    for c in range(CH):
                        dve.wait_ge(silu_done, CH * f + c + 1)
                        dve.wait_ge(up_done, CH * f + c + 1)
                        dve.tensor_tensor(hid[:, par, c, :], up_bank[c], silu[:, c, :],
                                          ALU.mult).then_inc(hid_done, 1)
                        if c == 0 and past(n):
                            residual(n - 1)
                    if f0 == 0 and isinstance(n, int) and n == 0:
                        inverse(1, KT, TILES)
                    if not (isinstance(n, int) and n >= NBLK - 2):
                        norm(n + 2, l0 + n + 2, par)

                return step, residual

            def x_stats(first, blocks):
                for n in blocks:
                    ins = block_stats(n)
                link(ins)

            dve.wait_ge(x_loaded[0], 16)
            x_stats(0, range(2))
            variance(0, KT)
            dve.wait_ge(ffn_w_loaded, 16 * 3)
            dve.tensor_scalar(w_gate[:, :], wi[:, 0, :], SCALE_INT8, None, ALU.mult)
            dve.tensor_scalar(w_up[:, :], wi[:, 1, :], SCALE_INT8, None, ALU.mult)
            dve.tensor_scalar(w_down[:, :, :].rearrange("p c d -> p (c d)"), wi[:, 2, :], SCALE_INT8, None,
                              ALU.mult).then_inc(weights_ready, 1)
            inverse(0, 0, KT)
            norm(0, 0, 0)
            norm(1, 1, 1)
            dve.wait_ge(x_loaded[1], 16 * (BATCH - 1))
            x_stats(1, range(2, NBLK))
            variance(KT, TILES)
            step, residual = ffn(0, 0, True)
            run_blocks(dve, step)

            dve.wait_ge(stats_done, NBLK - 1)
            variance(0, TILES - BT)
            inverse(2, 0, TILES - BT)
            norm(0, NBLK, 0)
            residual(NBLK - 1)
            dve.wait_ge(stats_done, NBLK)
            variance(TILES - BT, TILES)
            inverse(3, TILES - BT, TILES)
            norm(1, NBLK + 1, 1)

            def qkv_step(n, par, b):
                for t, bank in ((0, q_bank[par]), (1, k_bank[par])):
                    dve.wait_ge(hi_done, 2 * n + t + 1)
                    if t == 1 and past(n - 1):
                        dve.wait_ge(k_low_done, n - 1)
                    dve.scalar_tensor_tensor(resid[:, par, t, :], bank, b_qk[:, t:t + 1],
                                             parts[:, par, t, 0, :], ALU.add,
                                             ALU.subtract).then_inc(resid_done, 1)
                dve.wait_ge(resid_done, 2 * n + 1)
                dve.tensor_copy(parts[:, par, 0, 1, :], resid[:, par, 0, :]).then_inc(q_mid_done, 1)
                dve.wait_ge(q_mid_done, n + 1)
                dve.tensor_tensor(parts[:, par, 0, 2, :], resid[:, par, 0, :], parts[:, par, 0, 1, :],
                                  ALU.subtract).then_inc(q_low_done, 1)
                if not (isinstance(n, int) and n >= NBLK - 2):
                    norm(n + 2, NBLK + n + 2, par)

            dve.wait_ge(attn_w_loaded, 16 * 5)
            run_blocks(dve, qkv_step)

            def maxima(v, half, s):
                if s == 0 and past(v - 1):
                    dve.wait_ge(m_split, v - 1)
                for h in range(2):
                    dve.wait_ge(a_ready, 2 * BT * v + 2 * s + h + 1)
                    dve.tensor_reduce(nmax[:, half, h, s:s + 1], ps_a[h][:, :, :], AX.XY, ALU.max,
                                      negate=True).then_inc(max_done, 1)

            def read_max(r, v, v_pair, v_half):
                dve.wait_ge(misc_ready, r + 1)
                if past(v_pair):
                    dve.wait_ge(m_loaded[v_half], 16 * 2 * v_pair)
                dve.tensor_copy(m_rows[:, v_half, :], m_psum).then_inc(m_rows_ready, 1)

            def read_sums(r):
                dve.wait_ge(misc_ready, r + 1)
                dve.reciprocal(o_inv[:, :, :].rearrange("p b (h q) -> p b h q", h=2),
                               o_psum[:, :, :, :, DH]).then_inc(inv_done, 1)

            def write_rows(w, w_pair, w_half):
                dve.wait_ge(inv_done, w + 1)
                for h in range(2):
                    dst = att[:, bass.ds(w_pair, 1), w_half * BT:(w_half + 1) * BT, h * DH:(h + 1) * DH]
                    ins = dve.tensor_tensor(
                        dst.rearrange("p o (q b) e -> p b (o q) e", b=2), o_psum[:, :, h, :, 0:DH],
                        o_inv[:, :, 2 * h:2 * h + 2].unsqueeze(3).broadcast_to((P, 2, 2, DH)), ALU.mult)
                ins.then_inc(misc_read, 1)

            for s in range(STEPS):
                maxima(0, 0, s)
            maxima(1, 1, 0)
            maxima(1, 1, 1)
            read_max(0, 0, 0, 0)
            dve.wait_ge(m_rows_ready, 1)
            dve.sem_inc(misc_read, 1)
            maxima(1, 1, 2)
            maxima(1, 1, 3)

            def pair(p):
                last = isinstance(p, int) and p == PAIRS - 1
                first = isinstance(p, int) and p == 0
                for half in range(2):
                    u = 2 * p + half
                    before = not (first and half == 0)
                    for s in range(STEPS):
                        if not last:
                            maxima(u + 2, half, s)
                        if s == 1:
                            if not (last and half == 1):
                                read_max(u + 1, u + 1, p + half, 1 - half)
                            if before:
                                read_sums(u + 1)
                            else:
                                dve.wait_ge(m_rows_ready, u + 2)
                                dve.sem_inc(misc_read, 1)
                        if s == 2 and before:
                            write_rows(u - 1, p + half - 1, 1 - half)

            pair(0)
            with dve.Fori(1, PAIRS - 1) as p:
                pair(p)
            pair(PAIRS - 1)
            read_sums(2 * PAIRS + 1)
            write_rows(2 * PAIRS - 1, PAIRS - 1, 1)

            def proj_step(n, par, b):
                rows = x[:, bass.ds(BT * n, BT), :].rearrange("p t d -> p (t d)")
                dve.wait_ge(proj_done, n + 1)
                dve.tensor_tensor(rows, ps_a[par][:, 0, :], rows, ALU.add).then_inc(proj_added, 1)
                dve.wait_ge(proj_added, n + 1)
                block_stats(n).then_inc(stats_done, 1)

            def first_variance():
                dve.wait_ge(stats_done, 2 * NBLK - 2)
                variance(0, TILES - 2 * BT)

            dve.wait_ge(bias_added, 1)
            run_blocks(dve, proj_step, before_last=first_variance)

            inverse(4, 0, TILES - 2 * BT)
            norm(0, 2 * NBLK, 0)
            norm(1, 2 * NBLK + 1, 1)
            dve.wait_ge(stats_done, 2 * NBLK)
            variance(TILES - 2 * BT, TILES)
            inverse(5, TILES - 2 * BT, TILES)
            step, residual = ffn(NBLK, 2 * NBLK, False)
            run_blocks(dve, step)
            residual(NBLK - 1)

        @block.tensor
        def _(pe):
            def transpose_xn(L, par):
                pe.wait_ge(xn_ready, L + 1)
                if past(L):
                    pe.wait_ge(xT_copied, L)
                for j in range(BT):
                    mm = pe.transpose(ps_m[:, j * P:(j + 1) * P], xn[:, par, j, :], ident[:, :])
                mm.then_inc(xT_done, 1)

            def ffn(f0, l0):
                def hidden(n, par, c):
                    f = f0 + n
                    free = CH * f + c + 1 - CH
                    if c == 0:
                        pe.wait_ge(xT_copied, l0 + n + 1)
                    if past(free):
                        pe.wait_ge(silu_done, free)
                    pe.matmul(gate_bank[c], w_gate[:, c * P:(c + 1) * P], xT[:, par, :],
                              start=True, stop=True).then_inc(gate_done, 1)
                    if past(free):
                        pe.wait_ge(hid_done, free)
                    pe.matmul(up_bank[c], w_up[:, c * P:(c + 1) * P], xT[:, par, :],
                              start=True, stop=True).then_inc(up_done, 1)

                def down(n, par):
                    f = f0 + n
                    pe.wait_ge(hid_done, CH * (f + 1))
                    if past(f):
                        pe.wait_ge(res_done, f)
                    for j in range(BT):
                        for c in range(CH):
                            mm = pe.matmul(ps_o[:, j * P:(j + 1) * P], hid[:, par, c, j * P:(j + 1) * P],
                                           w_down[:, c, :], start=(c == 0), stop=(c == CH - 1))
                    mm.then_inc(down_done, 1)

                def step(n, par, b):
                    hidden(n, par, 0)
                    if past(n):
                        down(n - 1, 1 - par)
                    hidden(n, par, 1)
                    if not (isinstance(n, int) and n == NBLK - 1):
                        transpose_xn(l0 + n + 1, 1 - par)
                    hidden(n, par, 2)

                run_blocks(pe, step)
                down(NBLK - 1, 1)

            pe.wait_ge(consts_set, 2)
            transpose_xn(0, 0)
            pe.wait_ge(weights_ready, 1)
            ffn(0, 0)
            transpose_xn(NBLK, 0)

            def qkv_step(n, par, b):
                pe.wait_ge(xT_copied, NBLK + n + 1)
                if past(n - 1):
                    pe.wait_ge(resid_done, 2 * (n - 1))
                pe.matmul(q_bank[par], w_qkv[:, 0:DIM], xT[:, par, :], start=True, stop=True).then_inc(q_done, 1)
                pe.matmul(k_bank[par], w_qkv[:, DIM:2 * DIM], xT[:, par, :],
                          start=True, stop=True).then_inc(k_done, 1)
                if not (isinstance(n, int) and n == NBLK - 1):
                    transpose_xn(NBLK + n + 1, 1 - par)
                if past(n - 1):
                    pe.wait_ge(v_copied, n - 1)
                for j in range(BT):
                    mm = pe.matmul(v_bank[par][:, j * P:(j + 1) * P], xT[:, par, j * P:(j + 1) * P],
                                   w_qkv[:, 2 * DIM:3 * DIM], start=True, stop=True)
                mm.then_inc(v_done, 1)

            pe.wait_ge(attn_w_loaded, 16 * 5)
            run_blocks(pe, qkv_step)

            def scores_a(v, c, half, s, h, kh):
                q0 = half * UQ + s * P
                index = 2 * BT * v + 2 * s + h
                if kh == 0 and past(index - 1):
                    pe.wait_ge(max_done, index - 1)
                mm = pe.matmul(ps_a[h][:, kh, :], q_stack[0:QK_ROWS, c, h, q0:q0 + P],
                               k_stack[0:QK_ROWS, c, h, kh * 512:(kh + 1) * 512], start=True, stop=True)
                if kh == 1:
                    mm.then_inc(a_ready, 1)

            def scores_b(u, c, half, s, i):
                kt, h = 2 * s + i // 2, i % 2
                index = 4 * (STEPS * u + s) + i
                if past(index - 1):
                    pe.wait_ge(exp_done, index - 1)
                pe.matmul(ps_b[h][:, :], k_stack[0:ALL_ROWS, c, h, kt * P:(kt + 1) * P],
                          q_stack[0:ALL_ROWS, c, h, half * UQ:(half + 1) * UQ],
                          start=True, stop=True).then_inc(s_ready, 1)

            def pv(u, p, c, s, k):
                pe.wait_ge(exp_done, 4 * (STEPS * u + s) + 2 * k + 2)
                if s == 0 and k == 0:
                    pe.wait_ge(v_staged, p + 1)
                    if past(u):
                        pe.wait_ge(o_copied, u)
                kt = 2 * s + k
                for h in range(2):
                    for q in range(2):
                        j = 2 * h + q
                        mm = pe.matmul(ps_o[VW * j:VW * (j + 1), 0:256], v_stage[:, c, kt, h, :],
                                       probs[:, s % 2, 2 * k + h, q * 256:(q + 1) * 256],
                                       start=(kt == 0), stop=(kt == KT - 1))
                if k == 1:
                    mm.then_inc(pv_done, 1)

            def shared_round(r, v, v_half, w):
                if past(r):
                    pe.wait_ge(misc_read, r)
                if w is not None:
                    pe.wait_ge(o_copied, w + 1)
                    for b in range(2):
                        mm = pe.transpose(ps_m[:, b * P:(b + 1) * P], o_sb[:, b * P:(b + 1) * P], ident[:, :])
                if v is not None:
                    pe.wait_ge(m_split, v + 1)
                    mm = pe.transpose(m_psum, m_parts[:, v_half].rearrange("p h i t -> p (h i t)"), ident_b[:, :])
                mm.then_inc(misc_ready, 1)

            pe.wait_ge(v_copied, NBLK)
            pe.wait_ge(resid_done, 2 * NBLK)
            for v in range(2):
                if v == 0:
                    pe.wait_ge(qk_loaded[0], 16 * LOADS)
                for s in range(STEPS):
                    if v == 1 and s == 2:
                        shared_round(0, 0, 0, None)
                    for h in range(2):
                        for kh in range(2):
                            scores_a(v, 0, v, s, h, kh)

            def pair(p, c, turn):
                last = isinstance(p, int) and p == PAIRS - 1
                first = isinstance(p, int) and p == 0
                nxt = (c + 1) % NBUF
                for half in range(2):
                    u = 2 * p + half
                    pe.wait_ge(m_loaded[half], 16 * 2 * (p + 1))
                    if half == 0 and not last:
                        pe.wait_ge(qk_loaded[nxt], 16 * LOADS * (turn + (1 if c < NBUF - 1 else 2)))
                    for s in range(STEPS):
                        for i in range(4):
                            if not last:
                                scores_a(u + 2, nxt, half, s, i // 2, i % 2)
                            scores_b(u, c, half, s, i)
                            if i % 2 == 0:
                                if s > 0:
                                    pv(u, p, c, s - 1, i // 2)
                                elif half == 1:
                                    pv(u - 1, p, c, STEPS - 1, i // 2)
                                elif not first:
                                    pv(u - 1, p - 1, (c - 1) % NBUF, STEPS - 1, i // 2)
                        if s == 1:
                            shared_round(u + 1, None if last and half == 1 else u + 1, 1 - half,
                                         None if first and half == 0 else u - 1)

            run_pairs(pe, pair, 4)
            for k in range(2):
                pv(2 * PAIRS - 1, PAIRS - 1, (PAIRS - 1) % NBUF, STEPS - 1, k)
            shared_round(2 * PAIRS + 1, None, None, 2 * PAIRS - 1)

            def transpose_att(n, par):
                pe.wait_ge(staged, n + 1)
                if past(n - 1):
                    pe.wait_ge(attT_copied, n - 1)
                for j in range(BT):
                    mm = pe.transpose(ps_b[par][:, j * P:(j + 1) * P], att_stage[:, par, j, :], ident[:, :])
                mm.then_inc(attT_done, 1)

            def proj_step(n, par, b):
                if not (isinstance(n, int) and n == NBLK - 1):
                    transpose_att(n + 1, 1 - par)
                pe.wait_ge(attT_copied, n + 1)
                if past(n - 1):
                    pe.wait_ge(proj_added, n - 1)
                for j in range(BT):
                    mm = pe.matmul(ps_a[par][:, 0, j * P:(j + 1) * P], attT[:, par, j * P:(j + 1) * P], w_out[:, :],
                                   start=True, stop=True)
                mm.then_inc(proj_done, 1)

            pe.wait_ge(misc_read, 2 * PAIRS + 2)
            transpose_att(0, 0)
            run_blocks(pe, proj_step)
            transpose_xn(2 * NBLK, 0)
            pe.wait_ge(proj_added, NBLK)
            ffn(NBLK, 2 * NBLK)


def kernel(L0_attn_x, L0_attn_qkv_w, L0_attn_qkv_b, L0_attn_out_w, L0_attn_out_b, L0_ffn_w_gate, L0_ffn_w_up,
           L0_ffn_w_down):
    import numpy as np
    import concourse.bacc as bacc
    from concourse.bass_utils import run_bass_kernel_spmd as run

    w_qk = np.asarray(L0_attn_qkv_w)[:2 * DIM].reshape(2, HP, 2, DH, DIM).transpose(0, 1, 3, 2, 4)
    w_all = np.concatenate([w_qk.reshape(2 * DIM, DIM), np.asarray(L0_attn_qkv_w)[2 * DIM:]])
    b_qk = np.asarray(L0_attn_qkv_b)[:2 * DIM].reshape(2, HP, 2, DH).transpose(0, 1, 3, 2)
    arrays = {
        "x_in": np.ascontiguousarray(L0_attn_x).reshape(ROWS, DIM),
        "wqkv_t": np.ascontiguousarray(w_all.T),
        "qk_b": np.ascontiguousarray(b_qk.reshape(2, DIM).T),
        "v_b": np.ascontiguousarray(np.asarray(L0_attn_qkv_b)[2 * DIM:]),
        "wo_t": np.ascontiguousarray(np.asarray(L0_attn_out_w).T),
        "out_b": np.ascontiguousarray(L0_attn_out_b),
        "wg_t": np.ascontiguousarray(np.asarray(L0_ffn_w_gate).T),
        "wu_t": np.ascontiguousarray(np.asarray(L0_ffn_w_up).T),
        "wd_t": np.ascontiguousarray(np.asarray(L0_ffn_w_down).T),
    }
    nc = bacc.Bacc("TRN2", target_bir_lowering=False, num_devices=1)
    args = [nc.dram_tensor(name, a.shape, mybir.dt.from_np(a.dtype), kind="ExternalInput").ap()
            for name, a in arrays.items()]
    out = nc.dram_tensor("out", (ROWS, DIM), F32, kind="ExternalOutput").ap()
    macaron(nc, *args, out)
    r = run(nc, [arrays], core_ids=[0])
    return r.results[0]["out"].reshape(BATCH, SEQ, DIM)
```

```python
from contextlib import ExitStack

import concourse.bass as bass
from concourse import mybir

ALU = mybir.AluOpType
ACT = mybir.ActivationFunctionType
AX = mybir.AxisListType
F32 = mybir.dt.float32
BF16 = mybir.dt.bfloat16
I32 = mybir.dt.int32

P = 128
BATCH, SEQ, DIM = 4, 1024, 128
HEADS = 16
DH = DIM // HEADS
HID = 384
SCALE_INT8 = 1.0 / 127.0
SCALE_QK = float(DH) ** -0.5
EPS = 1e-5

ROWS = BATCH * SEQ
TILES = ROWS // P
BLK = 512
BT = BLK // P
NBLK = ROWS // BLK
CH = HID // P
GH = 4
BG = HEADS // GH
GROUPS = BATCH * BG
UQ = 512
KT = SEQ // P
STEPS = KT
LEAD = 3
O_STEP = 2
M_STEP = 5
PARTS = 3
QK_ROWS = PARTS * PARTS * DH
ALL_ROWS = QK_ROWS + PARTS
THIRD_BANK = [s for s in range(STEPS) if s not in (O_STEP + 1, M_STEP + 1)]
PROJ_STEPS = (1, 2, 4, 5, 6, 8, 9)
EARLY = TILES // 2
STD_STEP, XT_STEP = 5, 6
WARM_UP = 20
NBUF = 2
VW = 32
LOADS = 1 + PARTS


def past(count):
    return not isinstance(count, int) or count > 0


def run_blocks(eng, step, after_first=None, first=None):
    if first:
        first()
    else:
        step(0, 0, 0)
    if after_first:
        after_first()
    step(1, 1, 0)
    with eng.Fori(1, NBLK // 2 - 1) as i:
        step(2 * i, 0, i)
        step(2 * i + 1, 1, i)
    step(NBLK - 2, 0, NBLK // 2 - 1)
    step(NBLK - 1, 1, NBLK // 2 - 1)


def run_groups(eng, step):
    step(0, 0, 0)
    step(1, 1, 0)
    with eng.Fori(1, GROUPS // NBUF - 1) as i:
        for k in range(NBUF):
            step(i * NBUF + k, k, i)
    step(GROUPS - 2, 0, GROUPS // NBUF - 1)
    step(GROUPS - 1, 1, GROUPS // NBUF - 1)


def tail_step(last, half, s):
    z = STEPS * half + s - (STEPS - LEAD)
    return z if last and z >= 0 else None


def macaron(nc, x_in, wqkv_t, qk_b, v_b, wo_t, out_b, wg_t, wu_t, wd_t, out):
    with ExitStack() as ctx:
        def sb(name, shape, dt):
            return ctx.enter_context(nc.sbuf_tensor(name, shape, dt))

        def psum(name, shape):
            return ctx.enter_context(nc.psum_tensor(name, shape, F32))

        def sem(name):
            return ctx.enter_context(nc.semaphore(name))

        q_scr = nc.dram_tensor("q_parts_scratch", [GROUPS, PARTS, DH, GH, SEQ], BF16).ap()
        k_scr = nc.dram_tensor("k_parts_scratch", [GROUPS, PARTS, DH, GH, SEQ], BF16).ap()

        x = sb("x", [P, TILES, DIM], F32)
        stats = sb("stats", [P, TILES, 6], F32)
        mean = sb("mean", [P, TILES], F32)
        rstd = sb("rstd", [P, TILES], F32)
        ln_a = sb("ln_a", [P, TILES], F32)
        ln_b = sb("ln_b", [P, TILES], F32)
        ln_c = sb("ln_c", [P, TILES], F32)
        ln_d = sb("ln_d", [P, TILES], F32)
        eps = sb("eps", [P, 1], F32)
        xn = sb("xn", [P, 2, BT, DIM], F32)
        xT = sb("xT", [P, 2, BLK], F32)
        wi = sb("wi", [P, 3, HID], I32)
        w_gate = sb("w_gate", [P, HID], F32)
        w_up = sb("w_up", [P, HID], F32)
        w_down = sb("w_down", [P, CH, DIM], F32)
        w_qkv = sb("w_qkv", [P, 3 * DIM], F32)
        w_out = sb("w_out", [P, DIM], F32)
        b_qk = sb("b_qk", [P, 2], F32)
        b_v = sb("b_v", [P, 1], F32)
        b_out = sb("b_out", [P, DIM], F32)
        ident = sb("ident", [P, P], F32)
        ident_b = sb("ident_b", [P, P], BF16)
        silu = sb("silu", [P, CH, BLK], F32)
        hid = sb("hid", [P, 2, CH, BLK], F32)
        parts = sb("parts", [P, BATCH, 2, PARTS, SEQ], BF16)
        resid = sb("resid", [P, 2, 2, BLK], F32)
        v_all = sb("v_all", [P, GROUPS, KT, GH * DH], F32)
        v_stage = sb("v_stage", [P, NBUF, KT, GH, VW], F32)
        q_stack = sb("q_stack", [P, NBUF, GH, SEQ], BF16)
        k_stack = sb("k_stack", [P, NBUF, GH, SEQ], BF16)
        probs = sb("probs", [P, 2, GH, UQ], F32)
        nmax = sb("nmax", [P, 2, GH, BT], F32)
        zero = sb("zero", [P, 1], F32)
        m_res = sb("m_res", [P, GH, BT], F32)
        m_parts = sb("m_parts", [P, 2, GH, PARTS, BT], BF16)
        m_rows = sb("m_rows", [2 * PARTS * BT, 2, 2, P], BF16)
        o_sb = sb("o_sb", [P, UQ], F32)
        o_inv = sb("o_inv", [P, BT, GH], F32)
        att = (parts[:, 0:2].rearrange("p b t i r -> p (b t i r)").bitcast(F32)[:, 0:ROWS]
               .rearrange("p (g k e) -> p g k e", g=GROUPS, k=KT))
        att_stage = sb("att_stage", [P, 2, BT, DIM], F32)
        attT = sb("attT", [P, 2, BLK], F32)

        def block_part(b, par, t, i):
            return parts[:, bass.ds(b, 1), t, i, par * BLK:(par + 1) * BLK].rearrange("p o r -> p (o r)")

        ps_a = [psum(f"ps_a{h}", [P, 2, 512]) for h in range(2)]
        ps_b = [psum(f"ps_b{h}", [P, 512]) for h in range(2)]
        ps_o = psum("ps_o", [P, 512])
        ps_m = psum("ps_m", [P, 512])
        gate_bank = [ps_a[0][:, 0, :], ps_a[1][:, 0, :], ps_b[0][:, :]]
        up_bank = [ps_a[0][:, 1, :], ps_a[1][:, 1, :], ps_b[1][:, :]]
        q_bank = [ps_a[0][:, 0, :], ps_a[0][:, 1, :]]
        k_bank = [ps_a[1][:, 0, :], ps_a[1][:, 1, :]]
        v_bank = [ps_b[0][:, :], ps_b[1][:, :]]

        def b_bank(s, h):
            return ps_m if h == GH - 1 and s in THIRD_BANK else ps_b[h % 2]

        def attT_bank(n):
            return ps_a[1][:, n % 2, :] if n < NBLK - 1 else ps_b[0][:, :]

        def proj_bank(n):
            return ps_a[0][:, n % 2, :] if n < NBLK - 1 else ps_b[1][:, :]

        m_psum = ps_m[:, :].bitcast(BF16)[0:2 * PARTS * BT, 0:2 * P]
        o_psum = ps_m[:, :].rearrange("p (q h c) -> p q h c", q=BT, h=GH)

        x_loaded = [sem(f"x_loaded{i}") for i in range(3)]
        ffn_w_loaded = sem("ffn_w_loaded")
        attn_w_loaded = sem("attn_w_loaded")
        consts_set = sem("consts_set")
        zeroed = sem("zeroed")
        weights_ready = sem("weights_ready")
        stats_done = sem("stats_done")
        ln_chain = sem("ln_chain")
        var_ready = sem("var_ready")
        std_ready = sem("std_ready")
        xn_ready = sem("xn_ready")
        xT_done = sem("xT_done")
        xT_copied = sem("xT_copied")
        gate_done = sem("gate_done")
        up_done = sem("up_done")
        silu_done = sem("silu_done")
        hid_done = sem("hid_done")
        down_done = sem("down_done")
        res_done = sem("res_done")
        q_done = sem("q_done")
        k_done = sem("k_done")
        v_done = sem("v_done")
        v_copied = sem("v_copied")
        hi_done = sem("hi_done")
        resid_done = sem("resid_done")
        q_mid_done = sem("q_mid_done")
        k_mid_done = sem("k_mid_done")
        q_low_done = sem("q_low_done")
        k_low_done = sem("k_low_done")
        stored = sem("stored")
        qk_loaded = [sem(f"qk_loaded{i}") for i in range(NBUF)]
        v_staged = sem("v_staged")
        a_ready = sem("a_ready")
        max_done = sem("max_done")
        split_chain = sem("split_chain")
        m_split = sem("m_split")
        m_transposed = sem("m_transposed")
        m_rows_ready = sem("m_rows_ready")
        m_loaded = [sem(f"m_loaded{i}") for i in range(2)]
        s_ready = sem("s_ready")
        exp_done = sem("exp_done")
        pv_done = sem("pv_done")
        o_copied = sem("o_copied")
        o_transposed = sem("o_transposed")
        inv_done = sem("inv_done")
        rows_written = sem("rows_written")
        bias_added = sem("bias_added")
        staged = sem("staged")
        last_staged = sem("last_staged")
        attT_done = sem("attT_done")
        attT_copied = sem("attT_copied")
        proj_done = sem("proj_done")
        proj_added = sem("proj_added")
        out_stored = sem("out_stored")

        block = ctx.enter_context(nc.Block())

        @block.sync
        def _(sp):
            x_t = x_in.rearrange("(t p) d -> p t d", p=P)
            for k, (lo, hi) in enumerate(((0, BT), (BT, KT), (KT, TILES))):
                sp.dma_start(x[:, lo:hi, :], x_t[:, lo:hi, :]).then_inc(x_loaded[k], 16)
                if k == 0:
                    sp.dma_start(wi[:, 0, :], wg_t).then_inc(ffn_w_loaded, 16)
                    sp.dma_start(wi[:, 1, :], wu_t).then_inc(ffn_w_loaded, 16)
                    sp.dma_start(wi[:, 2, :].rearrange("p (c d) -> p c d", c=CH),
                                 wd_t.rearrange("(c p) d -> p c d", p=P)).then_inc(ffn_w_loaded, 16)

            def store(b):
                for t, scr, ready in ((0, q_scr, q_low_done), (1, k_scr, k_low_done)):
                    sp.wait_ge(ready, 2 * b + 2)
                    for i in range(PARTS):
                        dst = scr[bass.ds(BG * b, BG), i].rearrange("g d h t -> g (d h) t")
                        sp.dma_start(dst, parts[:, bass.ds(b, 1), t, i, :].rearrange("p o r -> p (o r)"))\
                            .then_inc(stored, 16)

            def load_stacks(g, c):
                k_parts = k_scr[bass.ds(g, 1)].rearrange("o i d h t -> o (i d) (h t)")
                sp.dma_start(k_stack[0:QK_ROWS, c, :, :],
                             k_parts.broadcast_to((PARTS, PARTS * DH, GH * SEQ))).then_inc(qk_loaded[c], 16)
                for i in range(PARTS):
                    lo = i * PARTS * DH
                    q_part = q_scr[bass.ds(g, 1), i].rearrange("o d h t -> o d (h t)")
                    sp.dma_start(q_stack[lo:lo + PARTS * DH, c, :, :],
                                 q_part.broadcast_to((PARTS, DH, GH * SEQ))).then_inc(qk_loaded[c], 16)

            store(0)
            sp.wait_ge(stored, 16 * 2 * PARTS)
            sp.wait_ge(zeroed, 1)
            load_stacks(0, 0)
            with sp.Fori(1, BATCH) as b:
                store(b)
            sp.wait_ge(stored, 16 * 2 * PARTS * BATCH)
            load_stacks(1, 1)

            def load_max(v, half, c):
                sp.wait_ge(m_rows_ready, v + 1)
                for h in range(GH):
                    dst = q_stack[QK_ROWS:ALL_ROWS, c, h, half * UQ:(half + 1) * UQ]
                    lo = h % 2 * PARTS * BT
                    sp.dma_start(dst.rearrange("i (t q) -> i t q", t=BT),
                                 m_rows[lo:lo + PARTS * BT, half, h // 2, :]).then_inc(m_loaded[half], 16)

            load_max(0, 0, 0)

            def group(g, c, i):
                load_max(2 * g + 1, 1, c)
                if not (isinstance(g, int) and g == GROUPS - 1):
                    load_max(2 * g + 2, 0, 1 - c)
                if not (isinstance(g, int) and g + NBUF >= GROUPS):
                    sp.wait_ge(s_ready, GH * STEPS * 2 * (g + 1))
                    load_stacks(g + NBUF, c)

            run_groups(sp, group)

            out_t = out.rearrange("(t p) d -> p t d", p=P)

            def write(n, par, b):
                sp.wait_ge(res_done, NBLK + n + 1)
                sp.dma_start(out_t[:, bass.ds(BT * n, BT), :],
                             x[:, bass.ds(BT * n, BT), :]).then_inc(out_stored, 16)

            run_blocks(sp, write)
            sp.wait_ge(out_stored, 16 * NBLK)

        @block.gpsimd
        def _(pool):
            pool.memset(ident[:], 0.0).then_inc(split_chain, 1)
            pool.memset(ident_b[:], 0.0).then_inc(split_chain, 1)
            pool.wait_ge(split_chain, 2)
            pool.affine_select(out=ident[:], in_=ident[:], compare_op=ALU.not_equal, fill=1.0, base=0,
                               pattern=[[-1, P]], channel_multiplier=1)
            pool.affine_select(out=ident_b[:], in_=ident_b[:], compare_op=ALU.not_equal, fill=1.0, base=0,
                               pattern=[[-1, P]], channel_multiplier=1).then_inc(consts_set, 1)
            pool.memset(v_stage[:], 0.0).then_inc(split_chain, 1)
            pool.wait_ge(split_chain, 3)
            pool.memset(v_stage[:, :, :, :, DH:DH + 1], 1.0)
            pool.memset(q_stack[:], 0.0)
            pool.memset(zero[:, :], 0.0)
            pool.memset(k_stack[:], 1.0).then_inc(zeroed, 1)

            def split_block(n, par, b):
                pool.wait_ge(resid_done, 2 * n + 2)
                pool.tensor_tensor(block_part(b, par, 1, 1), resid[:, par, 1, :],
                                   zero[:, :].broadcast_to((P, BLK)), ALU.add).then_inc(k_mid_done, 1)
                pool.wait_ge(k_mid_done, n + 1)
                pool.tensor_tensor(block_part(b, par, 1, 2), resid[:, par, 1, :], block_part(b, par, 1, 1),
                                   ALU.subtract).then_inc(k_low_done, 1)

            pool.wait_ge(zeroed, 1)
            run_blocks(pool, split_block)

            def stage_v(g, c):
                if past(g - NBUF + 1):
                    pool.wait_ge(pv_done, 2 * STEPS * (g - NBUF + 1))
                pool.tensor_tensor(v_stage[:, c, :, :, 0:DH],
                                   v_all[:, bass.ds(g, 1), :, :].rearrange("p o k (h d) -> p (o k) h d", h=GH),
                                   zero[:, :].unsqueeze(2).unsqueeze(3).broadcast_to((P, KT, GH, DH)),
                                   ALU.add).then_inc(v_staged, 1)

            def split_max(v, half):
                m, hi, mid, low = (nmax[:, half], m_parts[:, half, :, 0, :], m_parts[:, half, :, 1, :],
                                   m_parts[:, half, :, 2, :])
                pool.wait_ge(max_done, GH * BT * (v + 1))
                if past(v - 1):
                    pool.wait_ge(m_transposed, v - 1)
                z = zero[:, :].unsqueeze(2).broadcast_to((P, GH, BT))
                pool.tensor_tensor(hi, m, z, ALU.add).then_inc(split_chain, 1)
                pool.wait_ge(split_chain, 3 * v + 4)
                pool.tensor_tensor(m_res[:], m, hi, ALU.subtract).then_inc(split_chain, 1)
                pool.wait_ge(split_chain, 3 * v + 5)
                pool.tensor_tensor(mid, m_res[:], z, ALU.add).then_inc(split_chain, 1)
                pool.wait_ge(split_chain, 3 * v + 6)
                pool.tensor_tensor(low, m_res[:], mid, ALU.subtract).then_inc(m_split, 1)

            pool.wait_ge(v_copied, NBLK)
            stage_v(0, 0)
            split_max(0, 0)

            def group(g, c, i):
                last = isinstance(g, int) and g == GROUPS - 1
                if not last:
                    stage_v(g + 1, 1 - c)
                split_max(2 * g + 1, 1)
                if not last:
                    split_max(2 * g + 2, 0)

            pool.wait_ge(xn_ready, 2 * NBLK)
            pool.wait_ge(attn_w_loaded, 16 * 5)
            pool.tensor_tensor(x[:], x[:], b_out[:, :].unsqueeze(1).broadcast_to((P, TILES, DIM)),
                               ALU.add).then_inc(bias_added, 1)
            run_groups(pool, group)

            for n in range(NBLK - 1):
                pool.wait_ge(rows_written, 2 * BG * (n // 2) + 2 * BG - 1 + n % 2)
                if n >= 2:
                    pool.wait_ge(attT_done, n - 1)
                pool.tensor_tensor(att_stage[:, n % 2, :, :].rearrange("p t (g e) -> p t g e", g=BG),
                                   att[:, BG * (n // 2):BG * (n // 2 + 1), n % 2 * BT:(n % 2 + 1) * BT, :]
                                   .rearrange("p g t e -> p t g e"),
                                   zero[:, :].unsqueeze(2).unsqueeze(3).broadcast_to((P, BT, BG, GH * DH)),
                                   ALU.add).then_inc(staged, 1)

        @block.scalar
        def _(act):
            def load_attention_weights():
                act.dma_start(w_qkv[:, :], wqkv_t).then_inc(attn_w_loaded, 16)
                act.dma_start(w_out[:, :], wo_t).then_inc(attn_w_loaded, 16)
                act.dma_start(b_qk[:, :], qk_b).then_inc(attn_w_loaded, 16)
                act.dma_start(b_v[:, :], v_b.rearrange("(p o) -> p o", o=1)).then_inc(attn_w_loaded, 16)
                act.dma_start(b_out[:, :], out_b.rearrange("(o d) -> o d", o=1)
                              .broadcast_to((P, DIM))).then_inc(attn_w_loaded, 16)

            def std(k, lo, hi):
                act.wait_ge(var_ready, k + 1)
                act.activation(rstd[:, lo:hi], ln_a[:, lo:hi], ACT.Sqrt, bias=eps[:, 0:1]).then_inc(std_ready, 1)

            def copy_xT(L, par):
                act.wait_ge(xT_done, L + 1)
                act.copy(xT[:, par, :], ps_m[:, :]).then_inc(xT_copied, 1)

            def silu_chunk(f, c):
                act.wait_ge(gate_done, CH * f + c + 1)
                if past(CH * f + c + 1 - CH):
                    act.wait_ge(hid_done, CH * f + c + 1 - CH)
                act.activation(silu[:, c, :], gate_bank[c], ACT.Silu).then_inc(silu_done, 1)

            def ffn(f0, l0, after_first, first=None):
                def step(n, par, b):
                    for c in range(CH):
                        if c == CH - 1 and not (isinstance(n, int) and n == NBLK - 1):
                            copy_xT(l0 + n + 1, 1 - par)
                        silu_chunk(f0 + n, c)

                run_blocks(act, step, after_first, first)

            std(0, 0, BT)
            copy_xT(0, 0)
            std(1, BT, KT)
            load_attention_weights()
            ffn(0, 0, lambda: std(2, KT, TILES))
            std(3, 0, TILES - BT)
            copy_xT(NBLK, 0)
            std(4, TILES - BT, TILES)

            def qkv_step(n, par, b):
                if not (isinstance(n, int) and n == NBLK - 1):
                    copy_xT(NBLK + n + 1, 1 - par)
                for t, bank, done in ((0, q_bank[par], q_done), (1, k_bank[par], k_done)):
                    act.wait_ge(done, n + 1)
                    act.activation(block_part(b, par, t, 0), bank, ACT.Identity,
                                   bias=b_qk[:, t:t + 1]).then_inc(hi_done, 1)
                act.wait_ge(resid_done, 2 * n + 1)
                act.copy(block_part(b, par, 0, 1), resid[:, par, 0, :]).then_inc(q_mid_done, 1)
                v_dst = v_all[:, bass.ds(BG * b, BG), par * BT:(par + 1) * BT, :].rearrange("p g t e -> p t g e")
                act.wait_ge(v_done, n + 1)
                act.copy(v_dst, v_bank[par].rearrange("p (t g e) -> p t g e", t=BT, g=BG)).then_inc(v_copied, 1)

            act.wait_ge(attn_w_loaded, 16 * 5)
            run_blocks(act, qkv_step)

            def unit(u, half):
                last = isinstance(u, int) and u == 2 * GROUPS - 1
                for s in range(STEPS):
                    g = STEPS * u + s
                    if last and s == STD_STEP:
                        std(5, 0, EARLY)
                    if last and s == XT_STEP + 1:
                        copy_xT(2 * NBLK, 0)
                    for h in range(GH):
                        act.wait_ge(s_ready, GH * g + h + 1)
                        if h == 0 and past(g - 1):
                            act.wait_ge(pv_done, g - 1)
                        act.activation(probs[:, s % 2, h, :], b_bank(s, h)[:, :], ACT.Exp,
                                       scale=SCALE_QK).then_inc(exp_done, 1)

            for half in range(2):
                unit(half, half)
            with act.Fori(1, GROUPS - 1) as g:
                for half in range(2):
                    unit(2 * g + half, half)
            for half in range(2):
                unit(2 * GROUPS - 2 + half, half)

            def first_step():
                silu_chunk(NBLK, 0)
                act.wait_ge(rows_written, 2 * GROUPS)
                act.wait_ge(attT_done, NBLK - 2)
                act.copy(att_stage[:, 1, :, :].rearrange("p t (g e) -> p t g e", g=BG),
                         att[:, GROUPS - BG:GROUPS, BT:2 * BT, :]
                         .rearrange("p g t e -> p t g e")).then_inc(last_staged, 1)
                silu_chunk(NBLK, 1)
                act.wait_ge(attT_done, NBLK)
                act.wait_ge(proj_done, NBLK - 2)
                act.activation(attT[:, 1, :], ps_b[0][:, :], ACT.Identity, bias=b_v[:, 0:1]).then_inc(attT_copied, 1)
                copy_xT(2 * NBLK + 1, 1)
                silu_chunk(NBLK, 2)

            ffn(NBLK, 2 * NBLK, lambda: std(6, EARLY, TILES), first_step)

        @block.vector
        def _(dve):
            dve.memset(eps[:, :], EPS).then_inc(consts_set, 1)
            chain = [0]

            def link(ins):
                chain[0] += 1
                ins.then_inc(ln_chain, 1)
                dve.wait_ge(ln_chain, chain[0])

            def variance(lo, hi):
                t = slice(lo, hi)
                mean_e, ss_e, mean_o, ss_o = stats[:, t, 1], stats[:, t, 2], stats[:, t, 4], stats[:, t, 5]
                dve.tensor_tensor(ln_c[:, t], ss_e, ss_o, ALU.add)
                dve.tensor_tensor(ln_d[:, t], mean_e, mean_o, ALU.add)
                link(dve.tensor_tensor(ln_a[:, t], mean_e, mean_o, ALU.subtract))
                dve.tensor_scalar(mean[:, t], ln_d[:, t], 0.5, None, ALU.mult)
                link(dve.scalar_tensor_tensor(ln_b[:, t], ln_a[:, t], 0.25, ln_a[:, t], ALU.mult, ALU.mult))
                dve.scalar_tensor_tensor(ln_a[:, t], ln_c[:, t], 1.0 / DIM, ln_b[:, t], ALU.mult,
                                         ALU.add).then_inc(var_ready, 1)

            def inverse(k, lo, hi):
                dve.wait_ge(std_ready, k + 1)
                link(dve.reciprocal(rstd[:, lo:hi], rstd[:, lo:hi]))

            def norm(n, L, par):
                if past(L - 1):
                    dve.wait_ge(xT_done, L - 1)
                for j in range(BT):
                    t = BT * n + j
                    ins = dve.tensor_scalar(xn[:, par, j, :],
                                            x[:, bass.ds(t, 1), :].rearrange("p o d -> p (o d)"),
                                            mean[:, bass.ds(t, 1)], rstd[:, bass.ds(t, 1)],
                                            ALU.subtract, ALU.mult)
                ins.then_inc(xn_ready, 1)

            def block_stats(n):
                for j in range(BT):
                    t = BT * n + j
                    ins = dve.bn_stats(stats[:, bass.ds(t, 1), :].rearrange("p o s -> p (o s)"),
                                       x[:, bass.ds(t, 1), :].rearrange("p o d -> p (o d)"))
                return ins

            def gated(f, par, c):
                dve.wait_ge(silu_done, CH * f + c + 1)
                dve.wait_ge(up_done, CH * f + c + 1)
                dve.tensor_tensor(hid[:, par, c, :], up_bank[c], silu[:, c, :], ALU.mult).then_inc(hid_done, 1)

            def ffn(f0, l0, with_stats):
                def residual(n):
                    f = f0 + n
                    rows = x[:, bass.ds(BT * n, BT), :].rearrange("p t d -> p (t d)")
                    dve.wait_ge(down_done, f + 1)
                    dve.scalar_tensor_tensor(rows, ps_o[:, :], 0.5, rows, ALU.mult, ALU.add).then_inc(res_done, 1)
                    if with_stats:
                        dve.wait_ge(res_done, f + 1)
                        block_stats(n).then_inc(stats_done, 1)

                def step(n, par, b):
                    for c in range(CH):
                        gated(f0 + n, par, c)
                        if c == 0 and past(n):
                            residual(n - 1)
                    if f0 == 0 and isinstance(n, int) and n == 0:
                        inverse(2, KT, TILES)
                    if f0 > 0 and isinstance(n, int) and n == 1:
                        inverse(6, EARLY, TILES)
                    if not (isinstance(n, int) and n >= NBLK - 2):
                        norm(n + 2, l0 + n + 2, par)

                return step, residual

            def x_stats(blocks):
                for n in blocks:
                    ins = block_stats(n)
                link(ins)

            dve.wait_ge(x_loaded[0], 16)
            x_stats(range(1))
            variance(0, BT)
            dve.wait_ge(x_loaded[1], 16)
            x_stats(range(1, 2))
            inverse(0, 0, BT)
            norm(0, 0, 0)
            variance(BT, KT)
            dve.wait_ge(ffn_w_loaded, 16 * 3)
            dve.tensor_scalar(w_gate[:, :], wi[:, 0, :], SCALE_INT8, None, ALU.mult)
            dve.tensor_scalar(w_up[:, :], wi[:, 1, :], SCALE_INT8, None, ALU.mult)
            dve.tensor_scalar(w_down[:, :, :].rearrange("p c d -> p (c d)"), wi[:, 2, :], SCALE_INT8, None,
                              ALU.mult).then_inc(weights_ready, 1)
            inverse(1, BT, KT)
            norm(1, 1, 1)
            dve.wait_ge(x_loaded[2], 16)
            x_stats(range(2, NBLK))
            variance(KT, TILES)
            step, residual = ffn(0, 0, True)
            run_blocks(dve, step)

            dve.wait_ge(stats_done, NBLK - 1)
            variance(0, TILES - BT)
            inverse(3, 0, TILES - BT)
            norm(0, NBLK, 0)
            norm(1, NBLK + 1, 1)
            residual(NBLK - 1)
            dve.wait_ge(stats_done, NBLK)
            variance(TILES - BT, TILES)
            inverse(4, TILES - BT, TILES)

            def qkv_step(n, par, b):
                if not (isinstance(n, int) and n >= NBLK - 2):
                    norm(n + 2, NBLK + n + 2, par)
                for t, bank in ((0, q_bank[par]), (1, k_bank[par])):
                    dve.wait_ge(hi_done, 2 * n + t + 1)
                    if t == 1 and past(n - 1):
                        dve.wait_ge(k_low_done, n - 1)
                    dve.scalar_tensor_tensor(resid[:, par, t, :], bank, b_qk[:, t:t + 1],
                                             block_part(b, par, t, 0), ALU.add,
                                             ALU.subtract).then_inc(resid_done, 1)
                dve.wait_ge(q_mid_done, n + 1)
                dve.tensor_tensor(block_part(b, par, 0, 2), resid[:, par, 0, :], block_part(b, par, 0, 1),
                                  ALU.subtract).then_inc(q_low_done, 1)

            dve.wait_ge(attn_w_loaded, 16 * 5)
            run_blocks(dve, qkv_step)

            def maxima(v, half, s):
                if s == 0 and past(v - 1):
                    dve.wait_ge(m_split, v - 1)
                for j in range(2):
                    h, t = 2 * (s % 2) + j, s // 2
                    dve.wait_ge(a_ready, 2 * (STEPS * v + s) + j + 1)
                    dve.tensor_reduce(nmax[:, half, h, t:t + 1], ps_a[j][:, :, :], AX.XY, ALU.max,
                                      negate=True).then_inc(max_done, 1)

            def read_max(v, v_group, v_half):
                dve.wait_ge(m_transposed, v + 1)
                if past(v_group):
                    dve.wait_ge(m_loaded[v_half], 16 * GH * v_group)
                dve.tensor_copy(m_rows[:, v_half, :, :].rearrange("p h q -> p (h q)"), m_psum).then_inc(m_rows_ready, 1)

            def copy_o(u):
                dve.wait_ge(pv_done, STEPS * (u + 1))
                if past(u):
                    dve.wait_ge(o_transposed, u)
                dve.tensor_copy(o_sb[:, :], ps_o[:, :]).then_inc(o_copied, 1)

            def write_rows(w, w_group, w_half):
                dve.wait_ge(o_transposed, w + 1)
                dve.reciprocal(o_inv[:, :, :], o_psum[:, :, :, DH]).then_inc(inv_done, 1)
                dve.wait_ge(inv_done, w + 1)
                dst = att[:, bass.ds(w_group, 1), w_half * BT:(w_half + 1) * BT, :]
                dve.tensor_tensor(dst.rearrange("p o q (h e) -> p (o q) h e", h=GH), o_psum[:, :, :, 0:DH],
                                  o_inv[:, :, :].unsqueeze(3).broadcast_to((P, BT, GH, DH)),
                                  ALU.mult).then_inc(rows_written, 1)

            for s in range(STEPS):
                maxima(0, 0, s)
            for s in range(LEAD):
                if s == 1:
                    read_max(0, 0, 0)
                maxima(1, 1, s)

            def copy_attT(n):
                dve.wait_ge(attT_done, n + 1)
                if n >= 2:
                    dve.wait_ge(proj_done, n - 1)
                dve.tensor_scalar(attT[:, n % 2, :], ps_a[1][:, n % 2, :], b_v[:, 0:1], None,
                                  ALU.add).then_inc(attT_copied, 1)

            def add_projected(n):
                rows = x[:, BT * n:BT * (n + 1), :].rearrange("p t d -> p (t d)")
                dve.wait_ge(proj_done, n + 1)
                dve.tensor_tensor(rows, proj_bank(n), rows, ALU.add).then_inc(proj_added, 1)

            def row_stats(n):
                dve.wait_ge(proj_added, n + 1)
                block_stats(n).then_inc(stats_done, 1)

            def project(z):
                if z == 0:
                    dve.wait_ge(bias_added, 1)
                if z in PROJ_STEPS:
                    copy_attT(PROJ_STEPS.index(z))
                if z - 1 in PROJ_STEPS:
                    add_projected(PROJ_STEPS.index(z - 1))
                if z - 1 in PROJ_STEPS:
                    row_stats(PROJ_STEPS.index(z - 1))
                if z - 1 == PROJ_STEPS[EARLY // BT - 1]:
                    dve.wait_ge(stats_done, NBLK + EARLY // BT)
                    variance(0, EARLY)
                if z == STD_STEP + LEAD:
                    inverse(5, 0, EARLY)
                    norm(0, 2 * NBLK, 0)
                if z == XT_STEP + LEAD:
                    norm(1, 2 * NBLK + 1, 1)

            def group(g):
                last = isinstance(g, int) and g == GROUPS - 1
                for half in range(2):
                    u = 2 * g + half
                    for s in range(STEPS):
                        if s == 1 and not (isinstance(g, int) and u == 0):
                            copy_o(u - 1)
                        if s + LEAD < STEPS:
                            if not (last and half == 1):
                                maxima(u + 1, 1 - half, s + LEAD)
                        elif not last:
                            maxima(u + 2, half, s + LEAD - STEPS)
                        if s == O_STEP and not (isinstance(g, int) and u == 0):
                            write_rows(u - 1, g + half - 1, 1 - half)
                        if s == M_STEP and not (last and half == 1):
                            read_max(u + 1, g + half, 1 - half)
                        if tail_step(last, half, s) is not None:
                            project(tail_step(last, half, s))

            group(0)
            with dve.Fori(1, GROUPS - 1) as g:
                group(g)
            group(GROUPS - 1)
            copy_o(2 * GROUPS - 1)

            write_rows(2 * GROUPS - 1, GROUPS - 1, 1)

            def first_step():
                gated(NBLK, 0, 0)
                gated(NBLK, 0, 1)
                add_projected(NBLK - 1)
                row_stats(NBLK - 1)
                gated(NBLK, 0, 2)
                dve.wait_ge(stats_done, 2 * NBLK)
                variance(EARLY, TILES)
                norm(2, 2 * NBLK + 2, 0)

            step, residual = ffn(NBLK, 2 * NBLK, False)
            run_blocks(dve, step, first=first_step)
            residual(NBLK - 1)

        @block.tensor
        def _(pe):
            def transpose_xn(L, par):
                pe.wait_ge(xn_ready, L + 1)
                if past(L):
                    pe.wait_ge(xT_copied, L)
                for j in range(BT):
                    mm = pe.transpose(ps_m[:, j * P:(j + 1) * P], xn[:, par, j, :], ident[:, :])
                mm.then_inc(xT_done, 1)

            def ffn(f0, l0, first=None):
                def hidden(n, par, c):
                    f = f0 + n
                    free = CH * f + c + 1 - CH
                    if c == 0:
                        pe.wait_ge(xT_copied, l0 + n + 1)
                    if past(free):
                        pe.wait_ge(silu_done, free)
                    pe.matmul(gate_bank[c], w_gate[:, c * P:(c + 1) * P], xT[:, par, :],
                              start=True, stop=True).then_inc(gate_done, 1)
                    if past(free):
                        pe.wait_ge(hid_done, free)
                    pe.matmul(up_bank[c], w_up[:, c * P:(c + 1) * P], xT[:, par, :],
                              start=True, stop=True).then_inc(up_done, 1)

                def down(n, par):
                    f = f0 + n
                    pe.wait_ge(hid_done, CH * (f + 1))
                    if past(f):
                        pe.wait_ge(res_done, f)
                    for j in range(BT):
                        for c in range(CH):
                            mm = pe.matmul(ps_o[:, j * P:(j + 1) * P], hid[:, par, c, j * P:(j + 1) * P],
                                           w_down[:, c, :], start=(c == 0), stop=(c == CH - 1))
                    mm.then_inc(down_done, 1)

                def step(n, par, b):
                    hidden(n, par, 0)
                    if past(n):
                        down(n - 1, 1 - par)
                    hidden(n, par, 1)
                    if not (isinstance(n, int) and n == NBLK - 1):
                        transpose_xn(l0 + n + 1, 1 - par)
                    hidden(n, par, 2)

                run_blocks(pe, step, first=first and (lambda: first(hidden)))
                down(NBLK - 1, 1)

            pe.wait_ge(consts_set, 2)
            with pe.Fori(0, WARM_UP // 4):
                for j in range(4):
                    pe.matmul(ps_o[:, 0:P], ident[:, :], ident[:, :], start=True, stop=True)
            transpose_xn(0, 0)
            pe.wait_ge(weights_ready, 1)
            ffn(0, 0)
            transpose_xn(NBLK, 0)

            def qkv_step(n, par, b):
                pe.wait_ge(xT_copied, NBLK + n + 1)
                if not (isinstance(n, int) and n == NBLK - 1):
                    transpose_xn(NBLK + n + 1, 1 - par)
                if past(n - 1):
                    pe.wait_ge(resid_done, 2 * (n - 1))
                pe.matmul(q_bank[par], w_qkv[:, 0:DIM], xT[:, par, :], start=True, stop=True).then_inc(q_done, 1)
                pe.matmul(k_bank[par], w_qkv[:, DIM:2 * DIM], xT[:, par, :],
                          start=True, stop=True).then_inc(k_done, 1)
                if past(n - 1):
                    pe.wait_ge(v_copied, n - 1)
                for j in range(BT):
                    mm = pe.matmul(v_bank[par][:, j * P:(j + 1) * P], xT[:, par, j * P:(j + 1) * P],
                                   w_qkv[:, 2 * DIM:3 * DIM], start=True, stop=True)
                mm.then_inc(v_done, 1)

            pe.wait_ge(attn_w_loaded, 16 * 5)
            run_blocks(pe, qkv_step)

            def scores_a(v, c, half, s, j, kh):
                h, q0 = 2 * (s % 2) + j, half * UQ + s // 2 * P
                index = 2 * (STEPS * v + s) + j
                if kh == 0 and past(index - 1):
                    pe.wait_ge(max_done, index - 1)
                mm = pe.matmul(ps_a[j][:, kh, :], q_stack[0:QK_ROWS, c, h, q0:q0 + P],
                               k_stack[0:QK_ROWS, c, h, kh * 512:(kh + 1) * 512], start=True, stop=True)
                if kh == 1:
                    mm.then_inc(a_ready, 1)

            def scores_b(u, c, half, s, h):
                index = GH * (STEPS * u + s) + h
                third = h == GH - 1 and s in THIRD_BANK
                if third and past(index - 3):
                    pe.wait_ge(exp_done, index - 3)
                elif not third and past(index - 1):
                    pe.wait_ge(exp_done, index - 1)
                if third and isinstance(u, int) and u == 2 * GROUPS - 1 and s == XT_STEP + 1:
                    pe.wait_ge(xT_copied, 2 * NBLK + 1)
                if third and s == O_STEP + 2 and past(u):
                    pe.wait_ge(rows_written, u)
                if third and s == M_STEP + 2 and not (isinstance(u, int) and u == 2 * GROUPS - 1):
                    pe.wait_ge(m_rows_ready, u + 2)
                pe.matmul(b_bank(s, h)[:, :], k_stack[0:ALL_ROWS, c, h, s * P:(s + 1) * P],
                          q_stack[0:ALL_ROWS, c, h, half * UQ:(half + 1) * UQ],
                          start=True, stop=True).then_inc(s_ready, 1)

            def pv(u, g, c, s):
                pe.wait_ge(exp_done, GH * (STEPS * u + s + 1))
                if s == 0:
                    pe.wait_ge(v_staged, g + 1)
                    if past(u):
                        pe.wait_ge(o_copied, u)
                for h in range(GH):
                    mm = pe.matmul(ps_o[VW * h:VW * (h + 1), :], v_stage[:, c, s, h, :], probs[:, s % 2, h, :],
                                   start=(s == 0), stop=(s == STEPS - 1))
                mm.then_inc(pv_done, 1)

            def transpose_o(w):
                pe.wait_ge(o_copied, w + 1)
                if not (isinstance(w, int) and w == 2 * GROUPS - 1):
                    pe.wait_ge(exp_done, GH * (STEPS * (w + 1) + O_STEP + 1))
                if isinstance(w, int) and w == 2 * GROUPS - 1:
                    pe.wait_ge(rows_written, w)
                else:
                    pe.wait_ge(m_rows_ready, w + 2)
                for t in range(BT):
                    mm = pe.transpose(ps_m[:, t * P:(t + 1) * P], o_sb[:, t * P:(t + 1) * P], ident[:, :])
                mm.then_inc(o_transposed, 1)

            def transpose_max(v, v_half):
                pe.wait_ge(m_split, v + 1)
                if past(v):
                    pe.wait_ge(exp_done, GH * (STEPS * (v - 1) + M_STEP + 1))
                if past(v - 1):
                    pe.wait_ge(rows_written, v - 1)
                for j in range(2):
                    mm = pe.transpose(m_psum[:, j * P:(j + 1) * P],
                                      m_parts[:, v_half, 2 * j:2 * j + 2].rearrange("p h i t -> p (h i t)"),
                                      ident_b[:, :])
                mm.then_inc(m_transposed, 1)

            pe.wait_ge(resid_done, 2 * NBLK)
            pe.wait_ge(qk_loaded[0], 16 * LOADS)
            for n in range(STEPS + LEAD):
                if n == STEPS + 1:
                    transpose_max(0, 0)
                for j in range(2):
                    for kh in range(2):
                        scores_a(n // STEPS, 0, n // STEPS, n % STEPS, j, kh)
            pe.wait_ge(v_copied, NBLK)

            def transpose_att(n, ready, count):
                pe.wait_ge(ready, count)
                if n == 0:
                    pe.wait_ge(max_done, 2 * STEPS * 2 * GROUPS)
                if n >= 2:
                    pe.wait_ge(attT_copied, n - 1)
                for j in range(BT):
                    mm = pe.transpose(attT_bank(n)[:, j * P:(j + 1) * P], att_stage[:, n % 2, j, :], ident[:, :])
                mm.then_inc(attT_done, 1)

            def project(n):
                pe.wait_ge(attT_copied, n + 1)
                if n >= 2:
                    pe.wait_ge(proj_added, n - 1)
                for j in range(BT):
                    mm = pe.matmul(proj_bank(n)[:, j * P:(j + 1) * P], attT[:, n % 2, j * P:(j + 1) * P],
                                   w_out[:, :], start=True, stop=True)
                mm.then_inc(proj_done, 1)

            def group(g, c, turn):
                last = isinstance(g, int) and g == GROUPS - 1
                for half in range(2):
                    u = 2 * g + half
                    for s in range(STEPS):
                        a = s + LEAD
                        if a < STEPS:
                            v, v_c, v_half, exists = u + 1, (c + half) % NBUF, 1 - half, not (last and half == 1)
                        else:
                            v, v_c, v_half, exists = u + 2, 1 - c, half, not last
                        if a == STEPS and half == 0 and not last:
                            pe.wait_ge(qk_loaded[1 - c], 16 * LOADS * (turn + (1 if c == 0 else 2)))
                        if s == 0:
                            pe.wait_ge(m_loaded[half], 16 * GH * (g + 1))

                        def rows_max(j, kh):
                            if exists:
                                scores_a(v, v_c, v_half, a % STEPS, j, kh)

                        z = tail_step(last, half, s)
                        scores_b(u, c, half, s, 0)
                        rows_max(0, 0)
                        if z in PROJ_STEPS:
                            n = PROJ_STEPS.index(z)
                            transpose_att(n, staged, n + 1)
                        scores_b(u, c, half, s, 1)
                        rows_max(0, 1)
                        rows_max(1, 0)
                        if z is not None and z - 1 in PROJ_STEPS:
                            project(PROJ_STEPS.index(z - 1))
                        if last and half == 1 and s == XT_STEP:
                            transpose_xn(2 * NBLK, 0)
                        scores_b(u, c, half, s, 2)
                        rows_max(1, 1)
                        scores_b(u, c, half, s, 3)
                        if s > 0:
                            pv(u, g, c, s - 1)
                        elif half == 1:
                            pv(u - 1, g, c, STEPS - 1)
                        elif not (isinstance(g, int) and g == 0):
                            pv(u - 1, g - 1, 1 - c, STEPS - 1)
                        if s == O_STEP and not (isinstance(g, int) and u == 0):
                            transpose_o(u - 1)
                        if s == M_STEP and not (last and half == 1):
                            transpose_max(u + 1, 1 - half)

            run_groups(pe, group)
            pv(2 * GROUPS - 1, GROUPS - 1, 1, STEPS - 1)

            def first_step(hidden):
                pe.wait_ge(proj_added, NBLK - 1)
                hidden(0, 0, 0)
                transpose_o(2 * GROUPS - 1)
                hidden(0, 0, 1)
                transpose_att(NBLK - 1, last_staged, 1)
                transpose_xn(2 * NBLK + 1, 1)
                project(NBLK - 1)
                pe.wait_ge(proj_added, NBLK)
                hidden(0, 0, 2)

            ffn(NBLK, 2 * NBLK, first_step)


def kernel(L0_attn_x, L0_attn_qkv_w, L0_attn_qkv_b, L0_attn_out_w, L0_attn_out_b, L0_ffn_w_gate, L0_ffn_w_up,
           L0_ffn_w_down):
    import numpy as np
    import concourse.bacc as bacc
    from concourse.bass_utils import run_bass_kernel_spmd as run

    w_qk = np.asarray(L0_attn_qkv_w)[:2 * DIM].reshape(2, BG, GH, DH, DIM).transpose(0, 1, 3, 2, 4)
    w_all = np.concatenate([w_qk.reshape(2 * DIM, DIM), np.asarray(L0_attn_qkv_w)[2 * DIM:]])
    b_qk = np.asarray(L0_attn_qkv_b)[:2 * DIM].reshape(2, BG, GH, DH).transpose(0, 1, 3, 2)
    arrays = {
        "x_in": np.ascontiguousarray(L0_attn_x).reshape(ROWS, DIM),
        "wqkv_t": np.ascontiguousarray(w_all.T),
        "qk_b": np.ascontiguousarray(b_qk.reshape(2, DIM).T),
        "v_b": np.ascontiguousarray(np.asarray(L0_attn_qkv_b)[2 * DIM:]),
        "wo_t": np.ascontiguousarray(np.asarray(L0_attn_out_w).T),
        "out_b": np.ascontiguousarray(L0_attn_out_b),
        "wg_t": np.ascontiguousarray(np.asarray(L0_ffn_w_gate).T),
        "wu_t": np.ascontiguousarray(np.asarray(L0_ffn_w_up).T),
        "wd_t": np.ascontiguousarray(np.asarray(L0_ffn_w_down).T),
    }
    nc = bacc.Bacc("TRN2", target_bir_lowering=False, num_devices=1)
    args = [nc.dram_tensor(name, a.shape, mybir.dt.from_np(a.dtype), kind="ExternalInput").ap()
            for name, a in arrays.items()]
    out = nc.dram_tensor("out", (ROWS, DIM), F32, kind="ExternalOutput").ap()
    macaron(nc, *args, out)
    r = run(nc, [arrays], core_ids=[0])
    return r.results[0]["out"].reshape(BATCH, SEQ, DIM)
```
